# Optimizing a Trainium2 kernel written in Bass

```python
import numpy as np
import jax
import jax.numpy as jnp

def _softmax(x, axis=-1):
    return jax.nn.softmax(x, axis=axis)

def _gelu(x):
    return jax.nn.gelu(x, approximate=True)

def _silu(x):
    return jax.nn.silu(x)

def _sigmoid(x):
    return jax.nn.sigmoid(x)

def _layernorm(x, axis=-1, eps=1e-05):
    m = jnp.mean(x, axis=axis, keepdims=True)
    v = jnp.var(x, axis=axis, keepdims=True)
    return (x - m) / jnp.sqrt(v + eps)

def _scatter_add(tgt, idx, src, axis=0):
    return tgt.at[idx].add(src)

def _segment_sum(src, seg, n):
    return jax.ops.segment_sum(src, seg, n)
kernel_name = 'mk_dlrm_tower_d1_rec_r8_8725f2'

def setup_inputs(seed: int=0):
    np.random.seed(seed)
    _w = jnp.asarray

    def _rec_inputs():
        import jax
        import jax.numpy as jnp
        _tk = jax.random.key(seed)
        dense_ctx = jax.random.normal(jax.random.fold_in(_tk, 190), (1024, 16), jnp.float32)
        ids = jnp.stack([jax.random.randint(jax.random.fold_in(_tk, 200 + f), (1024,), 0, v, jnp.int32) for f, v in enumerate([1250, 1000, 1000, 1000, 125000, 1250, 12500, 1000, 1000, 12500, 1000, 12500, 12500, 12500, 1000, 1250, 1000, 125000, 1250, 1000, 12500, 12500, 12500, 1250, 125000, 1000, 125000, 1000, 12500, 125000, 1250, 1000])], axis=1)
        tbl_0 = 0.05 * jax.random.normal(jax.random.fold_in(_tk, 500 + 0), (1250, 16), jnp.float32)
        tbl_1 = 0.05 * jax.random.normal(jax.random.fold_in(_tk, 500 + 1), (1000, 16), jnp.float32)
        tbl_2 = 0.05 * jax.random.normal(jax.random.fold_in(_tk, 500 + 2), (1000, 16), jnp.float32)
        tbl_3 = 0.05 * jax.random.normal(jax.random.fold_in(_tk, 500 + 3), (1000, 16), jnp.float32)
        tbl_4 = 0.05 * jax.random.normal(jax.random.fold_in(_tk, 500 + 4), (125000, 16), jnp.float32)
        tbl_5 = 0.05 * jax.random.normal(jax.random.fold_in(_tk, 500 + 5), (1250, 16), jnp.float32)
        tbl_6 = 0.05 * jax.random.normal(jax.random.fold_in(_tk, 500 + 6), (12500, 16), jnp.float32)
        tbl_7 = 0.05 * jax.random.normal(jax.random.fold_in(_tk, 500 + 7), (1000, 16), jnp.float32)
        tbl_8 = 0.05 * jax.random.normal(jax.random.fold_in(_tk, 500 + 8), (1000, 16), jnp.float32)
        tbl_9 = 0.05 * jax.random.normal(jax.random.fold_in(_tk, 500 + 9), (12500, 16), jnp.float32)
        tbl_10 = 0.05 * jax.random.normal(jax.random.fold_in(_tk, 500 + 10), (1000, 16), jnp.float32)
        tbl_11 = 0.05 * jax.random.normal(jax.random.fold_in(_tk, 500 + 11), (12500, 16), jnp.float32)
        tbl_12 = 0.05 * jax.random.normal(jax.random.fold_in(_tk, 500 + 12), (12500, 16), jnp.float32)
        tbl_13 = 0.05 * jax.random.normal(jax.random.fold_in(_tk, 500 + 13), (12500, 16), jnp.float32)
        tbl_14 = 0.05 * jax.random.normal(jax.random.fold_in(_tk, 500 + 14), (1000, 16), jnp.float32)
        tbl_15 = 0.05 * jax.random.normal(jax.random.fold_in(_tk, 500 + 15), (1250, 16), jnp.float32)
        tbl_16 = 0.05 * jax.random.normal(jax.random.fold_in(_tk, 500 + 16), (1000, 16), jnp.float32)
        tbl_17 = 0.05 * jax.random.normal(jax.random.fold_in(_tk, 500 + 17), (125000, 16), jnp.float32)
        tbl_18 = 0.05 * jax.random.normal(jax.random.fold_in(_tk, 500 + 18), (1250, 16), jnp.float32)
        tbl_19 = 0.05 * jax.random.normal(jax.random.fold_in(_tk, 500 + 19), (1000, 16), jnp.float32)
        tbl_20 = 0.05 * jax.random.normal(jax.random.fold_in(_tk, 500 + 20), (12500, 16), jnp.float32)
        tbl_21 = 0.05 * jax.random.normal(jax.random.fold_in(_tk, 500 + 21), (12500, 16), jnp.float32)
        tbl_22 = 0.05 * jax.random.normal(jax.random.fold_in(_tk, 500 + 22), (12500, 16), jnp.float32)
        tbl_23 = 0.05 * jax.random.normal(jax.random.fold_in(_tk, 500 + 23), (1250, 16), jnp.float32)
        tbl_24 = 0.05 * jax.random.normal(jax.random.fold_in(_tk, 500 + 24), (125000, 16), jnp.float32)
        tbl_25 = 0.05 * jax.random.normal(jax.random.fold_in(_tk, 500 + 25), (1000, 16), jnp.float32)
        tbl_26 = 0.05 * jax.random.normal(jax.random.fold_in(_tk, 500 + 26), (125000, 16), jnp.float32)
        tbl_27 = 0.05 * jax.random.normal(jax.random.fold_in(_tk, 500 + 27), (1000, 16), jnp.float32)
        tbl_28 = 0.05 * jax.random.normal(jax.random.fold_in(_tk, 500 + 28), (12500, 16), jnp.float32)
        tbl_29 = 0.05 * jax.random.normal(jax.random.fold_in(_tk, 500 + 29), (125000, 16), jnp.float32)
        tbl_30 = 0.05 * jax.random.normal(jax.random.fold_in(_tk, 500 + 30), (1250, 16), jnp.float32)
        tbl_31 = 0.05 * jax.random.normal(jax.random.fold_in(_tk, 500 + 31), (1000, 16), jnp.float32)
        _rk = jax.random.fold_in(_tk, 7)
        W_top1 = 0.0693375 * jax.random.normal(jax.random.fold_in(_tk, 801), (208, 512), jnp.float32)
        W_top2 = 0.0441942 * jax.random.normal(jax.random.fold_in(_tk, 802), (512, 256), jnp.float32)
        W_top3 = 0.0625 * jax.random.normal(jax.random.fold_in(_tk, 803), (256, 1), jnp.float32)
        b_top1 = jnp.zeros((512,), jnp.float32)
        b_top2 = jnp.zeros((256,), jnp.float32)
        return (dense_ctx, ids, tbl_0, tbl_1, tbl_2, tbl_3, tbl_4, tbl_5, tbl_6, tbl_7, tbl_8, tbl_9, tbl_10, tbl_11, tbl_12, tbl_13, tbl_14, tbl_15, tbl_16, tbl_17, tbl_18, tbl_19, tbl_20, tbl_21, tbl_22, tbl_23, tbl_24, tbl_25, tbl_26, tbl_27, tbl_28, tbl_29, tbl_30, tbl_31, W_top1, b_top1, W_top2, b_top2, W_top3)
    dense_ctx, ids, tbl_0, tbl_1, tbl_2, tbl_3, tbl_4, tbl_5, tbl_6, tbl_7, tbl_8, tbl_9, tbl_10, tbl_11, tbl_12, tbl_13, tbl_14, tbl_15, tbl_16, tbl_17, tbl_18, tbl_19, tbl_20, tbl_21, tbl_22, tbl_23, tbl_24, tbl_25, tbl_26, tbl_27, tbl_28, tbl_29, tbl_30, tbl_31, W_top1, b_top1, W_top2, b_top2, W_top3 = _rec_inputs()

    def _L0_rec_setup():
        import jax, jax.numpy as jnp
        import numpy as np
        B, M, D = (2048, 32, 16)
        LAYERS = [64, 64, 64]
        key = jax.random.key(seed)
        ks = jax.random.split(key, 4)
        inp = {'embeddings': jax.random.normal(ks[0], (B, M, D), dtype=jnp.float32)}
        hk_1 = M
        for i, hk in enumerate(LAYERS):
            scale = (2.0 / (M * hk_1 + hk)) ** 0.5
            inp[f'W{i}'] = jax.random.normal(ks[i + 1], (M, hk_1, hk), dtype=jnp.float32) * scale
            hk_1 = hk
        return inp
    _L0_rec_all = _L0_rec_setup()
    _L0_rec_in = {k: v for k, v in _L0_rec_all.items() if k in ('W0', 'W1', 'W2')}
    del _L0_rec_all
    return {'dense_ctx': dense_ctx, 'ids': ids, 'tbl_0': tbl_0, 'tbl_1': tbl_1, 'tbl_2': tbl_2, 'tbl_3': tbl_3, 'tbl_4': tbl_4, 'tbl_5': tbl_5, 'tbl_6': tbl_6, 'tbl_7': tbl_7, 'tbl_8': tbl_8, 'tbl_9': tbl_9, 'tbl_10': tbl_10, 'tbl_11': tbl_11, 'tbl_12': tbl_12, 'tbl_13': tbl_13, 'tbl_14': tbl_14, 'tbl_15': tbl_15, 'tbl_16': tbl_16, 'tbl_17': tbl_17, 'tbl_18': tbl_18, 'tbl_19': tbl_19, 'tbl_20': tbl_20, 'tbl_21': tbl_21, 'tbl_22': tbl_22, 'tbl_23': tbl_23, 'tbl_24': tbl_24, 'tbl_25': tbl_25, 'tbl_26': tbl_26, 'tbl_27': tbl_27, 'tbl_28': tbl_28, 'tbl_29': tbl_29, 'tbl_30': tbl_30, 'tbl_31': tbl_31, 'W_top1': W_top1, 'b_top1': b_top1, 'W_top2': W_top2, 'b_top2': b_top2, 'W_top3': W_top3, 'L0_rec_W0': _L0_rec_in['W0'], 'L0_rec_W1': _L0_rec_in['W1'], 'L0_rec_W2': _L0_rec_in['W2']}

def reference(dense_ctx, ids, tbl_0, tbl_1, tbl_2, tbl_3, tbl_4, tbl_5, tbl_6, tbl_7, tbl_8, tbl_9, tbl_10, tbl_11, tbl_12, tbl_13, tbl_14, tbl_15, tbl_16, tbl_17, tbl_18, tbl_19, tbl_20, tbl_21, tbl_22, tbl_23, tbl_24, tbl_25, tbl_26, tbl_27, tbl_28, tbl_29, tbl_30, tbl_31, W_top1, b_top1, W_top2, b_top2, W_top3, L0_rec_W0, L0_rec_W1, L0_rec_W2):
    import jax
    import jax.numpy as jnp

    def _L0_rec_ref(embeddings, W0, W1, W2):
        import jax, jax.numpy as jnp
        import numpy as np
        B, M, D = (2048, 32, 16)
        LAYERS = [64, 64, 64]
        x0 = embeddings
        xk = x0
        outs = []
        for W in (W0, W1, W2):
            xk = jax.nn.relu(jnp.einsum('bmd,bhd,mhk->bkd', x0, xk, W))
            outs.append(jnp.sum(xk, axis=2))
        return jnp.concatenate(outs, axis=1)
    e = jnp.stack([tbl_0[ids[:, 0]], tbl_1[ids[:, 1]], tbl_2[ids[:, 2]], tbl_3[ids[:, 3]], tbl_4[ids[:, 4]], tbl_5[ids[:, 5]], tbl_6[ids[:, 6]], tbl_7[ids[:, 7]], tbl_8[ids[:, 8]], tbl_9[ids[:, 9]], tbl_10[ids[:, 10]], tbl_11[ids[:, 11]], tbl_12[ids[:, 12]], tbl_13[ids[:, 13]], tbl_14[ids[:, 14]], tbl_15[ids[:, 15]], tbl_16[ids[:, 16]], tbl_17[ids[:, 17]], tbl_18[ids[:, 18]], tbl_19[ids[:, 19]], tbl_20[ids[:, 20]], tbl_21[ids[:, 21]], tbl_22[ids[:, 22]], tbl_23[ids[:, 23]], tbl_24[ids[:, 24]], tbl_25[ids[:, 25]], tbl_26[ids[:, 26]], tbl_27[ids[:, 27]], tbl_28[ids[:, 28]], tbl_29[ids[:, 29]], tbl_30[ids[:, 30]], tbl_31[ids[:, 31]]], axis=1)
    z = _L0_rec_ref(e, L0_rec_W0, L0_rec_W1, L0_rec_W2)
    z = z.reshape(z.shape[0], -1)
    h = jnp.concatenate([z, dense_ctx], axis=1)
    h = jnp.maximum(h @ W_top1 + b_top1, 0.0)
    h = jnp.maximum(h @ W_top2 + b_top2, 0.0)
    y = h @ W_top3
    return y

_drawn_inputs = setup_inputs


def setup_inputs(seed=0):
    import zlib

    import numpy as np

    out = dict(_drawn_inputs(seed))
    spreads = {'b_top1': (0.0, 2.0), 'b_top2': (0.0, 0.8)}
    factors = {'tbl_0': 8.0,
     'tbl_1': 8.0,
     'tbl_2': 8.0,
     'tbl_3': 8.0,
     'tbl_4': 8.0,
     'tbl_5': 8.0,
     'tbl_6': 8.0,
     'tbl_7': 8.0,
     'tbl_8': 8.0,
     'tbl_9': 8.0,
     'tbl_10': 8.0,
     'tbl_11': 8.0,
     'tbl_12': 8.0,
     'tbl_13': 8.0,
     'tbl_14': 8.0,
     'tbl_15': 8.0,
     'tbl_16': 8.0,
     'tbl_17': 8.0,
     'tbl_18': 8.0,
     'tbl_19': 8.0,
     'tbl_20': 8.0,
     'tbl_21': 8.0,
     'tbl_22': 8.0,
     'tbl_23': 8.0,
     'tbl_24': 8.0,
     'tbl_25': 8.0,
     'tbl_26': 8.0,
     'tbl_27': 8.0,
     'tbl_28': 8.0,
     'tbl_29': 8.0,
     'tbl_30': 8.0,
     'tbl_31': 8.0,
     'L0_rec_W0': 3.611,
     'L0_rec_W1': 8.0,
     'L0_rec_W2': 8.0,
     'dense_ctx': 7.51}
    for name, (base, spread) in spreads.items():
        noise = np.random.default_rng([zlib.crc32(name.encode()), seed]).standard_normal(out[name].shape)
        drawn = base * np.exp(spread * noise) if base else spread * noise
        out[name] = jnp.asarray(drawn.astype(out[name].dtype))
    for name, factor in factors.items():
        out[name] = (out[name] * factor).astype(out[name].dtype)
    return out
```

```python
from contextlib import ExitStack

import numpy as np

import concourse.bass as bass
from concourse import mybir

F32 = mybir.dt.float32
I32 = mybir.dt.int32
U32 = mybir.dt.uint32
ALU = mybir.AluOpType
ACT = mybir.ActivationFunctionType
AX_X = mybir.AxisListType.X

P = 128
FIELDS = 32
DIM = 16
BATCH = 1024
MAPS = 64
TB = 128
TILES = BATCH // TB
HALF = 512
STREAM = 2 * HALF
COLS = TB * DIM
NCH = FIELDS * MAPS // P
BASES = [0, 4, 8, 12, 13, 1, 2, 3, 5, 6, 7, 9, 10, 11, 14, 15]
L0CH = 5
H1, H2 = 512, 256
DENSE = 16
ZD_ROWS = MAPS + DENSE

PHASES = [(0, 0), (1, 0), (0, 1), (1, 1), (0, 2), (1, 2)]
POOL_CHUNKS = [0, 0, 4, 2, 4, 2]
ZD_BUFS = 3
ZG_BUFS = 3
DMA_RING = 8192


def plan():
    phases, nd, ng = [], 0, 0
    for p, (_, layer) in enumerate(PHASES):
        n = L0CH if layer == 0 else NCH
        first_pool = n - POOL_CHUNKS[p]
        dve = [(j, min(2, first_pool - j)) for j in range(0, first_pool, 2)]
        pool = list(range(first_pool, n))
        dve_items = [("dve", nd + i, j, w) for i, (j, w) in enumerate(dve)]
        pool_items = [("pool", ng + i, j, 1) for i, j in enumerate(pool)]
        order, taken = [], 0
        for i, item in enumerate(dve_items):
            order.append(item)
            while taken < len(pool_items) and (taken + 1) * len(dve_items) <= (i + 1) * (len(pool_items) + 1):
                order.append(pool_items[taken])
                taken += 1
        order += pool_items[taken:]
        phases.append((dve_items, pool_items, order))
        nd += len(dve_items)
        ng += len(pool_items)
    return phases, nd, ng


PLAN, ND, NG = plan()
DVE_END = [sum(len(PLAN[q][0]) for q in range(p + 1)) for p in range(6)]
POOL_END = [sum(len(PLAN[q][1]) for q in range(p + 1)) for p in range(6)]


def ring_wait(t, n, per_tile, bufs):
    slot = n % bufs
    if n >= bufs:
        return slot, t * per_tile + (n - bufs + 1)
    last = max(x for x in range(per_tile) if x % bufs == slot)
    if isinstance(t, int) and t == 0:
        return slot, None
    return slot, (t - 1) * per_tile + (last + 1)


def build_cin_tower(nc, ids, dense_t, tables, w0a, w0b, w0c, w12, wtop1, btop1, wtop2, btop2, wtop3,
                    eye, eye2, out):
    with ExitStack() as ctx:
        def sb(name, shape, dt=F32):
            return ctx.enter_context(nc.sbuf_tensor(name, shape, dt))

        def psum(name, shape):
            return ctx.enter_context(nc.psum_tensor(name, shape, F32))

        def sem(name):
            return ctx.enter_context(nc.semaphore(name))

        rolled = sb("rolled", [P, NCH, COLS])
        zd = sb("zd", [P, ZD_BUFS, 2, STREAM])
        zg = sb("zg", [P, ZG_BUFS, STREAM])
        xk_sb = sb("xk_sb", [P, 2, STREAM])
        relu_ab = sb("relu_ab", [P, 2, HALF])
        x0t = sb("x0t", [P, FIELDS * DIM // P, TB])
        emb = sb("emb", [P, FIELDS * DIM])
        ids_sb = sb("ids_sb", [P, FIELDS], I32)
        w0 = sb("w0", [P, L0CH, MAPS])
        w0rev = sb("w0rev", [P, L0CH - 1, MAPS])
        w12_sb = sb("w12_sb", [P, 2, NCH, MAPS])
        wt1a = sb("wt1a", [P, H1])
        wt1b = sb("wt1b", [ZD_ROWS, H1])
        wt2 = sb("wt2", [P, H1 // P, H2])
        wt3 = sb("wt3", [P, H2 // P])
        bt1 = sb("bt1", [P, H1 // P])
        bt2 = sb("bt2", [P, H2 // P])
        eye_sb = sb("eye_sb", [P, P])
        eye2_sb = sb("eye2_sb", [P, MAPS])
        zpart = sb("zpart", [P, 3, 2, TB])
        z01 = sb("z01", [P, TB])
        z2d = sb("z2d", [ZD_ROWS, TB])
        h1 = sb("h1", [P, H1 // P, TB])
        h2 = sb("h2", [P, H2 // P, TB])
        y_sb = sb("y_sb", [1, TB])

        acc = psum("acc", [P, 2, HALF])
        xk_ps = psum("xk_ps", [P, 2, STREAM])
        stage = psum("stage", [P, FIELDS * DIM // P, TB])
        mlp = psum("mlp", [P, HALF])

        scratch = nc.dram_tensor("x0_scratch", [2, FIELDS, DIM, TB], F32, kind="Internal").ap()

        out_row = out.rearrange("b o -> o b")

        const_in = sem("const_in")
        const_count = 16 * 17
        w0_zeroed = sem("w0_zeroed")
        w0_ready = sem("w0_ready")
        ids_in = sem("ids_in")
        gathered = sem("gathered")
        transposed = sem("transposed")
        x0t_ready = sem("x0t_ready")
        base_in = [sem("base_x_in"), sem("base_y_in")]
        base_ps = sem("base_ps")
        scratch_in = sem("scratch_in")
        rolled_in = [[sem(f"rolled_{'xy'[s]}{j}_in") for j in range(NCH)] for s in range(2)]
        zd_ready = sem("zd_ready")
        zd_used = sem("zd_used")
        zg_ready = sem("zg_ready")
        zg_used = sem("zg_used")
        xk_ps_ready = sem("xk_ps_ready")
        xk_sb_ready = sem("xk_sb_ready")
        relu_ready = sem("relu_ready")
        reduced = sem("reduced")
        dense_in = sem("dense_in")
        zsum_done = sem("zsum_done")
        zsum_sb = sem("zsum_sb")
        h1_done = sem("h1_done")
        h1_sb = sem("h1_sb")
        h2_done = sem("h2_done")
        h2_sb = sem("h2_sb")
        y_done = sem("y_done")
        y_ready = sem("y_ready")
        out_done = sem("out_done")

        block = ctx.enter_context(nc.Block())

        def twice(x, w):
            return bass.AP(x.tensor, x.offset, [x.ap[0], [0, w], x.ap[-1]])

        @block.sync
        def _(sp):
            def known(value):
                return value if isinstance(value, int) else sp.snap(sp.to_reg(value))

            def at(t):
                return t * TB if isinstance(t, int) else sp.snap(t * TB)

            def load_ids(first):
                sp.dma_start(ids_sb[:, :], ids[bass.ds(first, TB), :]).then_inc(ids_in, 16)

            def load_dense(first):
                sp.dma_start(z2d[MAPS:ZD_ROWS, :], dense_t[:, bass.ds(first, TB)]).then_inc(dense_in, 16)

            def store_y(m):
                first = at(m)
                sp.wait_ge(y_ready, m + 1)
                sp.dma_start(out_row[:, bass.ds(first, TB)], y_sb[:, :]).then_inc(out_done, 16)

            def store_scratch(tiles):
                sp.wait_ge(x0t_ready, tiles)
                for copy in range(2):
                    sp.dma_start(scratch[copy].rearrange("(g f) d b -> (f d) g b", g=x0t.shape[1]),
                                 x0t[:, :, :]).then_inc(scratch_in, 16)

            def rows_from(first, s, step):
                return bass.AP(scratch.tensor, scratch.offset + first * COLS + s * STREAM,
                               [[COLS, FIELDS], [step * COLS, 4], [1, STREAM]])

            def load_base(s):
                sp.dma_start(xk_sb[:, s, :], rows_from(0, s, 0)).then_inc(base_in[s], 16)

            def load_rolled(s, j):
                sp.dma_start(rolled[:, j, s * STREAM:(s + 1) * STREAM],
                             rows_from(BASES[j], s, 1)).then_inc(rolled_in[s][j], 16)

            first = L0CH
            load_order = ([(0, j) for j in range(-1, first)] + [(1, j) for j in range(-1, first)]
                          + [(0, j) for j in range(first, NCH)] + [(1, j) for j in range(first, NCH)])

            load_ids(0)
            sp.dma_start(eye_sb[:, :], eye).then_inc(const_in, 16)
            sp.wait_ge(w0_zeroed, 2)
            sp.dma_start(w0[:, 0:L0CH - 1, :], w0a).then_inc(const_in, 16)
            sp.dma_start(w0rev[:, 1:, :], w0b[:, 1:, :]).then_inc(const_in, 16)
            for q in range(1, 4):
                sp.dma_start(w0rev[q:P:4, 0, :], w0b[q:P:4, 0, :]).then_inc(const_in, 16)
            sp.dma_start(w0[3:P:4, L0CH - 1, :], w0c).then_inc(const_in, 16)
            sp.dma_start(w12_sb[:, 0, :, :], w12[0]).then_inc(const_in, 16)
            sp.dma_start(w12_sb[:, 1, :, :], w12[1]).then_inc(const_in, 16)
            sp.dma_start(wt1a[:, :], wtop1[0:P, :]).then_inc(const_in, 16)
            sp.dma_start(wt1b[:, :], wtop1[P:P + ZD_ROWS, :]).then_inc(const_in, 16)
            sp.dma_start(wt2[:, :, :], wtop2.rearrange("(c p) n -> p c n", p=P)).then_inc(const_in, 16)
            sp.dma_start(wt3[:, :], wtop3).then_inc(const_in, 16)
            sp.dma_start(bt1[:, :], btop1).then_inc(const_in, 16)
            sp.dma_start(bt2[:, :], btop2).then_inc(const_in, 16)
            sp.dma_start(eye2_sb[:, :], eye2).then_inc(const_in, 16)
            sp.dma_start(z2d[MAPS:ZD_ROWS, :], dense_t[:, 0:TB]).then_inc(const_in, 16)
            sp.wait_ge(gathered, 16 * FIELDS)
            load_ids(TB)
            store_scratch(1)
            sp.wait_ge(scratch_in, 32)
            for s, j in load_order:
                if j < 0:
                    load_base(s)
                else:
                    load_rolled(s, j)

            def tile(t, ahead1=True, ahead2=True):
                if ahead2:
                    first = at(t + 2)
                    sp.wait_ge(gathered, 16 * FIELDS * (t + 2))
                    load_ids(first)
                if ahead1:
                    dve_count, pool_count, x0t_count = (
                        known(ND * t + DVE_END[3]), known(NG * t + POOL_END[3]), known(t + 2))
                    sp.wait_ge(zd_ready, dve_count)
                    sp.wait_ge(zg_ready, pool_count)
                    store_scratch(x0t_count)
                if not (isinstance(t, int) and t == 0):
                    first = at(t)
                    sp.wait_ge(h1_done, t)
                    load_dense(first)
                if ahead1:
                    freed = {}
                    for s in range(2):
                        dve_items, pool_items, _ = PLAN[4 + s]
                        for _, n, j, w in dve_items:
                            for c in range(w):
                                freed[(s, j + c)] = (zd_ready, ND * t + (n + 1))
                        for _, n, j, _ in pool_items:
                            freed[(s, j)] = (zg_ready, NG * t + (n + 1))
                    base_free = [known(NG * t + POOL_END[4 + s]) for s in range(2)]
                    sp.wait_ge(scratch_in, 32 * (t + 2))
                    for s, j in load_order:
                        if j < 0:
                            sp.wait_ge(zg_ready, base_free[s])
                            load_base(s)
                        else:
                            sp.wait_ge(*freed[(s, j)])
                            load_rolled(s, j)
                if not (isinstance(t, int) and t == 0):
                    store_y(t - 1)

            tile(0)
            with sp.Fori(1, TILES - 2) as t:
                tile(t)
            tile(TILES - 2, ahead2=False)
            tile(TILES - 1, ahead1=False, ahead2=False)
            store_y(TILES - 1)
            sp.wait_ge(out_done, 16 * TILES)

        @block.gpsimd
        def _(pool):
            def gather(f):
                pool.indirect_dma_start(emb[:, f * DIM:(f + 1) * DIM], None, tables[f],
                                        bass.IndirectOffsetOnAxis(ids_sb[:, f:f + 1].bitcast(U32), 0)
                                        ).then_inc(gathered, 16)

            def start_gathers(t):
                pool.wait_ge(ids_in, 16 * (t + 1))
                if not (isinstance(t, int) and t == 0):
                    pool.wait_ge(transposed, t)

            def product(t, p, n, j):
                s, layer = PHASES[p]
                slot, used = ring_wait(t, n, NG, ZG_BUFS)
                if used is not None:
                    pool.wait_ge(zg_used, used)
                if layer == 1:
                    pool.wait_ge(rolled_in[s][j], 16 * (t + 1))
                nc.gpsimd.tensor_tensor(zg[:, slot, :], rolled[:, j, s * STREAM:(s + 1) * STREAM],
                                        xk_sb[:, s, :], ALU.mult).then_inc(zg_ready, 1)

            start_gathers(0)
            for f in range(FIELDS):
                gather(f)
            start_gathers(1)
            for f in range(FIELDS):
                gather(f)

            def tile(t, ahead2=True):
                f = 0
                spread = NG - len(PLAN[2][1])
                for p in range(2, 6):
                    pool.wait_ge(xk_sb_ready, 16 * t + 4 * (p - 1))
                    for _, n, j, _ in PLAN[p][1]:
                        if ahead2 and n == len(PLAN[2][1]) - 1:
                            start_gathers(t + 2)
                        product(t, p, n, j)
                        if ahead2 and n >= len(PLAN[2][1]) - 1:
                            upto = -(-FIELDS * (n - len(PLAN[2][1]) + 2) // (spread + 1))
                            for f in range(f, upto):
                                gather(f)
                            f = upto

            tile(0)
            with pool.Fori(1, TILES - 2) as t:
                tile(t)
            tile(TILES - 2, ahead2=False)
            tile(TILES - 1, ahead2=False)

        @block.vector
        def _(dve):
            nc.vector.memset(w0[:, L0CH - 1, :], 0.0).then_inc(w0_zeroed, 1)
            nc.vector.memset(w0rev[:, 0, :], 0.0).then_inc(w0_zeroed, 1)
            dve.wait_ge(const_in, const_count)
            nc.vector.tensor_tensor(w0[:, 0:L0CH - 1, :], w0[:, 0:L0CH - 1, :], w0rev[:, :, :],
                                    ALU.add).then_inc(w0_ready, 1)

            def reduce_d(t, p):
                s, layer = PHASES[p]
                dve.wait_ge(relu_ready, 6 * t + (p + 1))
                nc.vector.tensor_reduce(zpart[:, layer, s, :],
                                        relu_ab[:, s, :].rearrange("p (d b) -> p b d", b=TB),
                                        AX_X, ALU.add).then_inc(reduced, 1)

            def tile(t):
                zero = isinstance(t, int) and t == 0
                y0 = DVE_END[0]
                x1 = DVE_END[1]
                y1 = DVE_END[2]
                x2 = DVE_END[3]
                y2 = DVE_END[4]
                reduces = {y0: (t - 1, 5), x1 + 4: (t, 0), y1: (t, 1), y1 + 3: (t, 2), x2 + 3: (t, 3),
                           y2 + 3: (t, 4)}
                for p, (s, layer) in enumerate(PHASES):
                    if layer == 0:
                        dve.wait_ge(base_ps, 4 * t + 2 * (s + 1))
                    else:
                        dve.wait_ge(xk_ps_ready, 16 * t + 4 * (p - 1))
                    for _, n, j, w in PLAN[p][0]:
                        slot, used = ring_wait(t, n, ND, ZD_BUFS)
                        if used is not None:
                            dve.wait_ge(zd_used, used)
                        for c in range(j, j + w):
                            if layer == 0 or (layer == 1 and c >= L0CH):
                                dve.wait_ge(rolled_in[s][c], 16 * (t + 1))
                        nc.vector.tensor_tensor(zd[:, slot, 0:w, :],
                                                rolled[:, j:j + w, s * STREAM:(s + 1) * STREAM],
                                                twice(xk_ps[:, s, :], w), ALU.mult).then_inc(zd_ready, 1)
                        if n in reduces and not (zero and reduces[n][1] == 5):
                            if reduces[n][1] == 0 and not zero:
                                dve.wait_ge(zsum_done, t)
                            reduce_d(*reduces[n])

            tile(0)
            with dve.Fori(1, TILES - 2) as t:
                tile(t)
            tile(TILES - 2)
            tile(TILES - 1)
            reduce_d(TILES - 1, 5)

        @block.scalar
        def _(act):
            def transposes_to_sb(t):
                act.wait_ge(transposed, t + 1)
                if not (isinstance(t, int) and t == 0):
                    act.wait_ge(scratch_in, 32 * t)
                nc.scalar.copy(x0t[:, :, :], stage[:, :, :]).then_inc(x0t_ready, 1)

            def base_to_ps(t, s):
                if not (isinstance(t, int) and t == 0):
                    act.wait_ge(zd_ready, ND * (t - 1) + DVE_END[4 + s])
                act.wait_ge(base_in[s], 16 * (t + 1))
                for h in range(2):
                    nc.scalar.copy(xk_ps[:, s, h * HALF:(h + 1) * HALF],
                                   xk_sb[:, s, h * HALF:(h + 1) * HALF]).then_inc(base_ps, 1)

            def evacuate(t, p):
                s, layer = PHASES[p]
                who, n, _, _ = PLAN[p][2][-1]
                if who == "dve":
                    act.wait_ge(zd_used, ND * t + (n + 1))
                else:
                    act.wait_ge(zg_used, NG * t + (n + 1))
                if layer < 2:
                    for dst, ready in ((xk_ps, xk_ps_ready), (xk_sb, xk_sb_ready)):
                        for h in range(2):
                            for copy in range(2):
                                nc.scalar.activation(
                                    dst[copy * MAPS:(copy + 1) * MAPS, s, h * HALF:(h + 1) * HALF],
                                    acc[h * MAPS:(h + 1) * MAPS, s, :], ACT.Relu).then_inc(ready, 1)
                if not (isinstance(t, int) and t == 0 and p < 2):
                    act.wait_ge(reduced, 6 * t + (p - 1))
                nc.scalar.activation(relu_ab[:, s, :], acc[:, s, :], ACT.Relu).then_inc(relu_ready, 1)

            def zsum_to_sb(m):
                act.wait_ge(zsum_done, m + 1)
                nc.scalar.copy(z01[:, :], mlp[:, 0:TB]).then_inc(zsum_sb, 1)
                nc.scalar.copy(z2d[0:MAPS, :], mlp[0:MAPS, TB:2 * TB]).then_inc(zsum_sb, 1)

            def h1_to_sb(m):
                act.wait_ge(h1_done, m + 1)
                for c in range(H1 // P):
                    nc.scalar.activation(h1[:, c, :], mlp[:, c * TB:(c + 1) * TB], ACT.Relu,
                                         bias=bt1[:, c:c + 1]).then_inc(h1_sb, 1)

            def h2_to_sb(m):
                act.wait_ge(h2_done, m + 1)
                for c in range(H2 // P):
                    nc.scalar.activation(h2[:, c, :], mlp[:, c * TB:(c + 1) * TB], ACT.Relu,
                                         bias=bt2[:, c:c + 1]).then_inc(h2_sb, 1)

            def y_to_sb(m):
                act.wait_ge(y_done, m + 1)
                if not (isinstance(m, int) and m == 0):
                    act.wait_ge(out_done, 16 * m)
                nc.scalar.copy(y_sb[:, :], mlp[0:1, 0:TB]).then_inc(y_ready, 1)

            act.wait_ge(const_in, const_count)
            transposes_to_sb(0)
            base_to_ps(0, 0)

            def tile(t, ahead1=True):
                zero = isinstance(t, int) and t == 0
                base_to_ps(t, 1)
                evacuate(t, 0)
                if ahead1:
                    transposes_to_sb(t + 1)
                evacuate(t, 1)
                if not zero:
                    zsum_to_sb(t - 1)
                evacuate(t, 2)
                if not zero:
                    h1_to_sb(t - 1)
                evacuate(t, 3)
                if not zero:
                    h2_to_sb(t - 1)
                evacuate(t, 4)
                if not zero:
                    y_to_sb(t - 1)
                if ahead1:
                    base_to_ps(t + 1, 0)
                evacuate(t, 5)

            tile(0)
            with act.Fori(1, TILES - 2) as t:
                tile(t)
            tile(TILES - 2)
            tile(TILES - 1, ahead1=False)
            zsum_to_sb(TILES - 1)
            h1_to_sb(TILES - 1)
            h2_to_sb(TILES - 1)
            y_to_sb(TILES - 1)

        @block.tensor
        def _(pe):
            def transpose(t):
                pe.wait_ge(gathered, 16 * FIELDS * (t + 1))
                if not (isinstance(t, int) and t == 0):
                    pe.wait_ge(x0t_ready, t)
                for g in range(FIELDS * DIM // P):
                    last = nc.tensor.transpose(stage[:, g, :], emb[:, g * P:(g + 1) * P], eye_sb[:, :])
                last.then_inc(transposed, 1)

            def phase(t, p):
                s, layer = PHASES[p]
                _, _, order = PLAN[p]
                if not (isinstance(t, int) and t == 0 and p < 2):
                    pe.wait_ge(relu_ready, 6 * t + (p - 1))
                for i, (who, n, j, w) in enumerate(order):
                    if who == "dve":
                        pe.wait_ge(zd_ready, ND * t + (n + 1))
                    else:
                        pe.wait_ge(zg_ready, NG * t + (n + 1))
                    for c in range(w):
                        weights = w0[:, j + c, :] if layer == 0 else w12_sb[:, layer - 1, j + c, :]
                        for h in range(2):
                            z = zd[:, n % ZD_BUFS, c, :] if who == "dve" else zg[:, n % ZG_BUFS, :]
                            last = nc.tensor.matmul(acc[h * MAPS:(h + 1) * MAPS, s, :], weights,
                                                    z[:, h * HALF:(h + 1) * HALF],
                                                    start=(i == 0 and c == 0),
                                                    stop=(i == len(order) - 1 and c == w - 1))
                    last.then_inc(zd_used if who == "dve" else zg_used, 1)

            def zsum(m):
                pe.wait_ge(reduced, 6 * (m + 1))
                if not (isinstance(m, int) and m == 0):
                    pe.wait_ge(y_ready, m)
                for dst, layer in ((mlp[0:MAPS, 0:TB], 0), (mlp[MAPS:P, 0:TB], 1), (mlp[0:MAPS, TB:2 * TB], 2)):
                    for s in range(2):
                        last = nc.tensor.matmul(dst, eye2_sb[:, :], zpart[:, layer, s, :],
                                                start=(s == 0), stop=(s == 1))
                last.then_inc(zsum_done, 1)

            def mlp1(m):
                pe.wait_ge(zsum_sb, 2 * (m + 1))
                if not (isinstance(m, int) and m == 0):
                    pe.wait_ge(dense_in, 16 * m)
                for c in range(H1 // P):
                    dst = mlp[:, c * TB:(c + 1) * TB]
                    nc.tensor.matmul(dst, wt1a[:, c * P:(c + 1) * P], z01[:, :], start=True, stop=False)
                    last = nc.tensor.matmul(dst, wt1b[:, c * P:(c + 1) * P], z2d[:, :], start=False, stop=True)
                last.then_inc(h1_done, 1)

            def mlp2(m):
                pe.wait_ge(h1_sb, 4 * (m + 1))
                for c in range(H2 // P):
                    for k in range(H1 // P):
                        last = nc.tensor.matmul(mlp[:, c * TB:(c + 1) * TB], wt2[:, k, c * P:(c + 1) * P],
                                                h1[:, k, :], start=(k == 0), stop=(k == H1 // P - 1))
                last.then_inc(h2_done, 1)

            def mlp3(m):
                pe.wait_ge(h2_sb, 2 * (m + 1))
                for k in range(H2 // P):
                    last = nc.tensor.matmul(mlp[0:1, 0:TB], wt3[:, k:k + 1], h2[:, k, :],
                                            start=(k == 0), stop=(k == H2 // P - 1))
                last.then_inc(y_done, 1)

            pe.wait_ge(const_in, const_count)
            transpose(0)
            pe.wait_ge(w0_ready, 1)

            def tile(t, ahead1=True):
                zero = isinstance(t, int) and t == 0
                phase(t, 0)
                if ahead1:
                    transpose(t + 1)
                phase(t, 1)
                if not zero:
                    zsum(t - 1)
                phase(t, 2)
                if not zero:
                    mlp1(t - 1)
                phase(t, 3)
                if not zero:
                    mlp2(t - 1)
                phase(t, 4)
                if not zero:
                    mlp3(t - 1)
                phase(t, 5)

            tile(0)
            with pe.Fori(1, TILES - 2) as t:
                tile(t)
            tile(TILES - 2)
            tile(TILES - 1, ahead1=False)
            zsum(TILES - 1)
            mlp1(TILES - 1)
            mlp2(TILES - 1)
            mlp3(TILES - 1)


def layout(inputs):
    p = np.arange(P)
    base = np.array(BASES)
    m = (base[:, None] + p[None, :] % 4 + p[None, :] // 4) % FIELDS
    h = np.broadcast_to(p % MAPS, m.shape)
    w12 = np.stack([np.asarray(inputs[f"L0_rec_W{n}"])[m, h].transpose(1, 0, 2) for n in (1, 2)])
    W0 = np.asarray(inputs["L0_rec_W0"])
    h0 = np.broadcast_to(p // 4, m.shape)
    w0a = W0[m, h0].transpose(1, 0, 2)[:, 0:L0CH - 1]
    w0b = W0[h0, m].transpose(1, 0, 2)[:, 0:L0CH - 1]
    w0c = W0[m, h0].transpose(1, 0, 2)[3:P:4, L0CH - 1]
    return {
        "ids": np.asarray(inputs["ids"]),
        "dense_t": np.asarray(inputs["dense_ctx"]).T,
        **{f"tbl_{f}": np.asarray(inputs[f"tbl_{f}"]) for f in range(FIELDS)},
        "w0a": w0a, "w0b": w0b, "w0c": w0c, "w12": w12,
        "wtop1": np.asarray(inputs["W_top1"]), "btop1": np.asarray(inputs["b_top1"]).reshape(-1, P).T,
        "wtop2": np.asarray(inputs["W_top2"]), "btop2": np.asarray(inputs["b_top2"]).reshape(-1, P).T,
        "wtop3": np.asarray(inputs["W_top3"]).reshape(-1, P).T,
        "eye": np.eye(P, dtype=np.float32), "eye2": np.tile(np.eye(MAPS, dtype=np.float32), (2, 1)),
    }


def kernel(**inputs):
    from concourse import bacc
    from concourse.bass_utils import run_bass_kernel_spmd

    arrays = {f"{k}_in": np.ascontiguousarray(v) for k, v in layout(inputs).items()}
    nc = bacc.Bacc("TRN2", target_bir_lowering=False, num_devices=1,
                   dynamic_dma_scratch_size=DMA_RING)
    aps = {k[:-3]: nc.dram_tensor(k, v.shape, mybir.dt.from_np(v.dtype), kind="ExternalInput").ap()
           for k, v in arrays.items()}
    out = nc.dram_tensor("y_out", (BATCH, 1), F32, kind="ExternalOutput").ap()
    tables = [aps.pop(f"tbl_{f}") for f in range(FIELDS)]
    build_cin_tower(nc, tables=tables, out=out, **aps)
    r = run_bass_kernel_spmd(nc, [arrays], core_ids=[0])
    return r.results[0]["y_out"]
```

```python
from contextlib import ExitStack

import numpy as np

import concourse.bass as bass
from concourse import mybir

F32 = mybir.dt.float32
I32 = mybir.dt.int32
U32 = mybir.dt.uint32
ALU = mybir.AluOpType
ACT = mybir.ActivationFunctionType
AX_X = mybir.AxisListType.X

P = 128
FIELDS = 32
DIM = 16
BATCH = 1024
MAPS = 64
TB = 128
TILES = BATCH // TB
HALF = 512
STREAM = 2 * HALF
COLS = TB * DIM
NCH = FIELDS * MAPS // P
BASES = [1, 5, 9, 13, 0, 2, 3, 4, 6, 7, 8, 10, 11, 12, 14, 15]
L0CH = 4
H1, H2 = 512, 256
DENSE = 16
ZD_ROWS = MAPS + DENSE

PHASES = [(0, 0), (1, 0), (0, 1), (1, 1), (0, 2), (1, 2)]
POOL_CHUNKS = [0, 0, 4, 2, 4, 2]
POOL_CHUNKS_FIRST = [0, 0, 0, 0, 4, 2]
ZD_BUFS = 3
ZG_BUFS = 4
GATHERS_NEXT = {3: 7, 5: 5}
GATHERS_LATER = {9: 2, 11: 18}
DMA_RING = 8192


class Plan:

    def __init__(self, pool_chunks, like=None):
        self.phases = []
        nd = ng = 0
        for p, (_, layer) in enumerate(PHASES):
            n = L0CH if layer == 0 else NCH
            first_pool = n - pool_chunks[p]
            dve = [("dve", nd + i, j, min(2, first_pool - j)) for i, j in enumerate(range(0, first_pool, 2))]
            pool = [("pool", ng + i, j, 1) for i, j in enumerate(range(first_pool, n))]
            order, taken = [], 0
            for i, item in enumerate(dve):
                order.append(item)
                while taken < len(pool) and (taken + 1) * len(dve) <= (i + 1) * (len(pool) + 1):
                    order.append(pool[taken])
                    taken += 1
            self.phases.append((dve, pool, order + pool[taken:]))
            nd += len(dve)
            ng += len(pool)
        self.total = {"dve": nd, "pool": ng}
        self.steady = self.total if like is None else like.total
        self.end = {who: [sum(len(x[k]) for x in self.phases[:p + 1]) for p in range(6)]
                    for k, who in enumerate(("dve", "pool"))}

    def slot(self, who, n):
        bufs = ZD_BUFS if who == "dve" else ZG_BUFS
        return (n + self.steady[who] - self.total[who]) % bufs


STEADY = Plan(POOL_CHUNKS)
FIRST = Plan(POOL_CHUNKS_FIRST, like=STEADY)


def is_first(t):
    return isinstance(t, int) and t == 0


def plan_of(t):
    return FIRST if is_first(t) else STEADY


def count(who, t, n):
    if is_first(t):
        return n
    return STEADY.total[who] * t + (FIRST.total[who] - STEADY.total[who] + n)


def freed_at(who, t, n):
    plan = plan_of(t)
    slot = plan.slot(who, n)
    before = [x for x in range(n) if plan.slot(who, x) == slot]
    if before:
        return count(who, t, before[-1] + 1)
    if is_first(t):
        return None
    last = max(x for x in range(STEADY.total[who]) if STEADY.slot(who, x) == slot)
    return count(who, t, last + 1 - STEADY.total[who])


def build_cin_tower(nc, ids, dense_t, tables, w0a, w0b, w0c, w12, wtop1, btop1, wtop2, btop2, wtop3,
                    eye, eye2, out):
    with ExitStack() as ctx:
        def sb(name, shape, dt=F32):
            return ctx.enter_context(nc.sbuf_tensor(name, shape, dt))

        def psum(name, shape):
            return ctx.enter_context(nc.psum_tensor(name, shape, F32))

        def sem(name):
            return ctx.enter_context(nc.semaphore(name))

        rolled = sb("rolled", [P, NCH, COLS])
        zd = sb("zd", [P, ZD_BUFS, 2, STREAM])
        zg = sb("zg", [P, ZG_BUFS, STREAM])
        xk_sb = sb("xk_sb", [P, 2, STREAM])
        relu_ab = sb("relu_ab", [P, 2, HALF])
        x0t = sb("x0t", [P, FIELDS * DIM // P, TB])
        emb = sb("emb", [P, FIELDS * DIM])
        ids_sb = sb("ids_sb", [P, TILES, FIELDS], I32)
        ids_tile = sb("ids_tile", [P, FIELDS], I32)
        w0 = sb("w0", [P, L0CH + 1, MAPS])
        w0rev = sb("w0rev", [P, L0CH, MAPS])
        w12_sb = sb("w12_sb", [P, 2, NCH, MAPS])
        wt1a = sb("wt1a", [P, H1])
        wt1b = sb("wt1b", [ZD_ROWS, H1])
        wt2 = sb("wt2", [P, H1 // P, H2])
        wt3 = sb("wt3", [P, H2 // P])
        bt1 = sb("bt1", [P, H1 // P])
        bt2 = sb("bt2", [P, H2 // P])
        eye_sb = sb("eye_sb", [P, P])
        eye2_sb = sb("eye2_sb", [P, MAPS])
        zpart = sb("zpart", [P, 3, 2, TB])
        z01 = sb("z01", [P, TB])
        z2d = sb("z2d", [ZD_ROWS, TB])
        h1 = sb("h1", [P, H1 // P, TB])
        h2 = sb("h2", [P, H2 // P, TB])
        y_sb = sb("y_sb", [1, TB])

        acc = psum("acc", [P, 2, HALF])
        xk_ps = psum("xk_ps", [P, 2, STREAM])
        stage = psum("stage", [P, FIELDS * DIM // P, TB])
        mlp = psum("mlp", [P, HALF])

        scratch = nc.dram_tensor("x0_scratch", [2, FIELDS, DIM, TB], F32, kind="Internal").ap()

        out_row = out.rearrange("b o -> o b")

        const_in = sem("const_in")
        const_count = 16 * 17
        w0_zeroed = sem("w0_zeroed")
        w0_ready = sem("w0_ready")
        ids_in = sem("ids_in")
        ids_copied = sem("ids_copied")
        gathered = sem("gathered")
        transposed = sem("transposed")
        x0t_ready = sem("x0t_ready")
        base_in = [sem("base_x_in"), sem("base_y_in")]
        base_ps = sem("base_ps")
        squares_ready = sem("squares_ready")
        scratch_in = sem("scratch_in")
        rolled_in = [[sem(f"rolled_{'xy'[s]}{j}_in") for j in range(NCH)] for s in range(2)]
        zd_ready = sem("zd_ready")
        zd_used = sem("zd_used")
        zg_ready = sem("zg_ready")
        zg_used = sem("zg_used")
        xk_ps_ready = sem("xk_ps_ready")
        xk_sb_ready = sem("xk_sb_ready")
        relu_ready = sem("relu_ready")
        reduced = sem("reduced")
        dense_in = sem("dense_in")
        zsum_done = sem("zsum_done")
        zsum_sb = sem("zsum_sb")
        h1_done = sem("h1_done")
        h1_sb = sem("h1_sb")
        h2_done = sem("h2_done")
        h2_sb = sem("h2_sb")
        y_done = sem("y_done")
        y_ready = sem("y_ready")
        out_done = sem("out_done")

        block = ctx.enter_context(nc.Block())

        def twice(x, w):
            return bass.AP(x.tensor, x.offset, [x.ap[0], [0, w], x.ap[-1]])

        @block.sync
        def _(sp):
            def known(value):
                return value if isinstance(value, int) else sp.snap(sp.to_reg(value))

            def at(t):
                return t * TB if isinstance(t, int) else sp.snap(t * TB)

            def load_dense(first):
                sp.dma_start(z2d[MAPS:ZD_ROWS, :], dense_t[:, bass.ds(first, TB)]).then_inc(dense_in, 16)

            def store_y(m):
                first = at(m)
                sp.wait_ge(y_ready, m + 1)
                sp.dma_start(out_row[:, bass.ds(first, TB)], y_sb[:, :]).then_inc(out_done, 16)

            def store_scratch(tiles):
                sp.wait_ge(x0t_ready, tiles)
                for copy in range(2):
                    sp.dma_start(scratch[copy].rearrange("(g f) d b -> (f d) g b", g=x0t.shape[1]),
                                 x0t[:, :, :]).then_inc(scratch_in, 16)

            def rows_from(first, s, step):
                return bass.AP(scratch.tensor, scratch.offset + first * COLS + s * STREAM,
                               [[COLS, FIELDS], [step * COLS, 4], [1, STREAM]])

            def load_base(s):
                sp.dma_start(xk_sb[:, s, :], rows_from(0, s, 0)).then_inc(base_in[s], 16)

            def load_rolled(s, j):
                sp.dma_start(rolled[:, j, s * STREAM:(s + 1) * STREAM],
                             rows_from(BASES[j], s, 1)).then_inc(rolled_in[s][j], 16)

            first = L0CH
            load_order = ([(0, j) for j in range(-1, first)] + [(1, j) for j in range(-1, first)]
                          + [(0, j) for j in range(first, NCH)] + [(1, j) for j in range(first, NCH)])

            sp.dma_start(ids_sb[:, 0, :], ids[0:TB, :]).then_inc(ids_in, 16)
            sp.dma_start(ids_sb[:, 1:, :], ids[TB:, :].rearrange("(t b) f -> b t f", b=TB)).then_inc(ids_in, 16)
            sp.dma_start(eye_sb[:, :], eye).then_inc(const_in, 16)
            sp.wait_ge(w0_zeroed, 2)
            sp.dma_start(w0[:, 0:L0CH, :], w0a).then_inc(const_in, 16)
            sp.dma_start(w0rev[:, 0:L0CH - 1, :], w0b[:, 0:L0CH - 1, :]).then_inc(const_in, 16)
            for q in range(3):
                sp.dma_start(w0rev[q:P:4, L0CH - 1, :], w0b[q:P:4, L0CH - 1, :]).then_inc(const_in, 16)
            sp.dma_start(w0[0:P:4, L0CH, :], w0c).then_inc(const_in, 16)
            sp.dma_start(w12_sb[:, 0, :, :], w12[0]).then_inc(const_in, 16)
            sp.dma_start(w12_sb[:, 1, :, :], w12[1]).then_inc(const_in, 16)
            sp.dma_start(wt1a[:, :], wtop1[0:P, :]).then_inc(const_in, 16)
            sp.dma_start(wt1b[:, :], wtop1[P:P + ZD_ROWS, :]).then_inc(const_in, 16)
            sp.dma_start(wt2[:, :, :], wtop2.rearrange("(c p) n -> p c n", p=P)).then_inc(const_in, 16)
            sp.dma_start(wt3[:, :], wtop3).then_inc(const_in, 16)
            sp.dma_start(bt1[:, :], btop1).then_inc(const_in, 16)
            sp.dma_start(bt2[:, :], btop2).then_inc(const_in, 16)
            sp.dma_start(eye2_sb[:, :], eye2).then_inc(const_in, 16)
            sp.dma_start(z2d[MAPS:ZD_ROWS, :], dense_t[:, 0:TB]).then_inc(const_in, 16)
            store_scratch(1)
            sp.wait_ge(scratch_in, 32)
            for s, j in load_order:
                if j < 0:
                    load_base(s)
                else:
                    load_rolled(s, j)

            def tile(t, ahead=True):
                if ahead:
                    dve_count, pool_count, x0t_count = (
                        known(count("dve", t, plan_of(t).end["dve"][3])),
                        known(count("pool", t, plan_of(t).end["pool"][3])), known(t + 2))
                    sp.wait_ge(zd_ready, dve_count)
                    sp.wait_ge(zg_ready, pool_count)
                    store_scratch(x0t_count)
                if not is_first(t):
                    first = at(t)
                    sp.wait_ge(h1_done, t)
                    load_dense(first)
                if ahead:
                    freed = {}
                    for s in range(2):
                        dve_items, pool_items, _ = plan_of(t).phases[4 + s]
                        for _, n, j, w in dve_items:
                            for c in range(w):
                                freed[(s, j + c)] = (zd_ready, count("dve", t, n + 1))
                        for _, n, j, _ in pool_items:
                            freed[(s, j)] = (zg_ready, count("pool", t, n + 1))
                    base_free = [known(count("pool", t, plan_of(t).end["pool"][4 + s])) for s in range(2)]
                    sp.wait_ge(scratch_in, 32 * (t + 2))
                    for s, j in load_order:
                        if j < 0:
                            sp.wait_ge(zg_ready, base_free[s])
                            load_base(s)
                        else:
                            sp.wait_ge(*freed[(s, j)])
                            load_rolled(s, j)
                if not is_first(t):
                    store_y(t - 1)

            tile(0)
            with sp.Fori(1, TILES - 2) as t:
                tile(t)
            tile(TILES - 2)
            tile(TILES - 1, ahead=False)
            store_y(TILES - 1)
            sp.wait_ge(out_done, 16 * TILES)

        @block.gpsimd
        def _(pool):
            def gather(index, f):
                pool.indirect_dma_start(emb[:, f * DIM:(f + 1) * DIM], None, tables[f],
                                        bass.IndirectOffsetOnAxis(index[:, f:f + 1].bitcast(U32), 0)
                                        ).then_inc(gathered, 16)

            def product(t, p, n, j):
                s, layer = PHASES[p]
                free = freed_at("pool", t, n)
                if free is not None:
                    pool.wait_ge(zg_used, free)
                if layer == 1 or is_first(t):
                    pool.wait_ge(rolled_in[s][j], 16 * (t + 1))
                nc.gpsimd.tensor_tensor(zg[:, plan_of(t).slot("pool", n), :],
                                        rolled[:, j, s * STREAM:(s + 1) * STREAM],
                                        xk_sb[:, s, :], ALU.mult).then_inc(zg_ready, 1)

            pool.wait_ge(ids_in, 32)
            for f in range(FIELDS):
                gather(ids_sb[:, 0, :], f)
            pool.wait_ge(transposed, 1)
            for f in range(FIELDS):
                gather(ids_sb[:, 1, :], f)

            def tile(t, later=True, following=True):
                plan = plan_of(t)
                start = min(GATHERS_LATER)
                for p in range(2, 6):
                    if plan.phases[p][1]:
                        pool.wait_ge(xk_sb_ready, 16 * t + 4 * (p - 1))
                    for _, n, j, _ in plan.phases[p][1]:
                        place = n + STEADY.total["pool"] - plan.total["pool"]
                        if later and place == start - 1:
                            pool.wait_ge(gathered, 16 * FIELDS * (t + 2))
                        if later and place == start:
                            pool.wait_ge(ids_copied, t + 1)
                            pool.wait_ge(transposed, t + 2)
                        product(t, p, n, j)
                        if later and place == start - 1:
                            nc.gpsimd.tensor_copy(ids_tile[:, :], ids_sb[:, t + 2, :]).then_inc(ids_copied, 1)
                        if following and place in GATHERS_NEXT:
                            done = sum(GATHERS_LATER.values()) + sum(
                                k for x, k in GATHERS_NEXT.items() if x < place)
                            for f in range(done, done + GATHERS_NEXT[place]):
                                gather(ids_tile, f)
                        if later and place in GATHERS_LATER:
                            done = sum(k for x, k in GATHERS_LATER.items() if x < place)
                            for f in range(done, done + GATHERS_LATER[place]):
                                gather(ids_tile, f)

            tile(0, following=False)
            with pool.Fori(1, TILES - 2) as t:
                tile(t)
            tile(TILES - 2, later=False)
            tile(TILES - 1, later=False, following=False)

        @block.vector
        def _(dve):
            nc.vector.memset(w0[:, L0CH, :], 0.0).then_inc(w0_zeroed, 1)
            nc.vector.memset(w0rev[:, L0CH - 1, :], 0.0).then_inc(w0_zeroed, 1)
            dve.wait_ge(const_in, const_count)
            nc.vector.tensor_tensor(w0[:, 0:L0CH, :], w0[:, 0:L0CH, :], w0rev[:, :, :],
                                    ALU.add).then_inc(w0_ready, 1)

            def reduce_d(t, p):
                s, layer = PHASES[p]
                dve.wait_ge(relu_ready, 6 * t + (p + 1))
                nc.vector.tensor_reduce(zpart[:, layer, s, :],
                                        relu_ab[:, s, :].rearrange("p (d b) -> p b d", b=TB),
                                        AX_X, ALU.add).then_inc(reduced, 1)

            def tile(t):
                y0, x1, y1, x2, y2 = plan_of(t).end["dve"][0:5]
                reduces = {y0 + 1: (t - 1, 5), x1 + 4: (t, 0), y1: (t, 1), y1 + 3: (t, 2), x2 + 3: (t, 3),
                           y2 + 3: (t, 4)}
                for p, (s, layer) in enumerate(PHASES):
                    if layer == 0:
                        dve.wait_ge(base_ps, 4 * t + 2 * (s + 1))
                    else:
                        dve.wait_ge(xk_ps_ready, 16 * t + 4 * (p - 1))
                    for _, n, j, w in plan_of(t).phases[p][0]:
                        free = freed_at("dve", t, n)
                        if free is not None:
                            dve.wait_ge(zd_used, free)
                        for c in range(j, j + w):
                            if layer == 0 or (layer == 1 and c >= L0CH):
                                dve.wait_ge(rolled_in[s][c], 16 * (t + 1))
                        nc.vector.tensor_tensor(zd[:, plan_of(t).slot("dve", n), 0:w, :],
                                                rolled[:, j:j + w, s * STREAM:(s + 1) * STREAM],
                                                twice(xk_ps[:, s, :], w), ALU.mult).then_inc(zd_ready, 1)
                        if n in reduces and not (is_first(t) and reduces[n][1] == 5):
                            if reduces[n][1] == 0 and not is_first(t):
                                dve.wait_ge(zsum_done, t)
                            reduce_d(*reduces[n])

            tile(0)
            with dve.Fori(1, TILES - 2) as t:
                tile(t)
            tile(TILES - 2)
            tile(TILES - 1)
            reduce_d(TILES - 1, 5)

        @block.scalar
        def _(act):
            def transposes_to_sb(t):
                act.wait_ge(transposed, t + 1)
                if not is_first(t):
                    act.wait_ge(scratch_in, 32 * t)
                nc.scalar.copy(x0t[:, :, :], stage[:, :, :]).then_inc(x0t_ready, 1)

            def base_to_ps(t, s):
                if not is_first(t):
                    act.wait_ge(zd_ready, count("dve", t, STEADY.end["dve"][4 + s] - STEADY.end["dve"][5]))
                act.wait_ge(base_in[s], 16 * (t + 1))
                for h in range(2):
                    nc.scalar.copy(xk_ps[:, s, h * HALF:(h + 1) * HALF],
                                   xk_sb[:, s, h * HALF:(h + 1) * HALF]).then_inc(base_ps, 1)
                act.wait_ge(base_ps, 4 * t + 2 * (s + 1))
                nc.scalar.activation(xk_sb[:, s, :], xk_sb[:, s, :], ACT.Square).then_inc(squares_ready, 1)

            def evacuate(t, p):
                s, layer = PHASES[p]
                who, n, _, _ = plan_of(t).phases[p][2][-1]
                act.wait_ge(zd_used if who == "dve" else zg_used, count(who, t, n + 1))
                if layer < 2:
                    for dst, ready in ((xk_ps, xk_ps_ready), (xk_sb, xk_sb_ready)):
                        for h in range(2):
                            for copy in range(2):
                                nc.scalar.activation(
                                    dst[copy * MAPS:(copy + 1) * MAPS, s, h * HALF:(h + 1) * HALF],
                                    acc[h * MAPS:(h + 1) * MAPS, s, :], ACT.Relu).then_inc(ready, 1)
                if not (is_first(t) and p < 2):
                    act.wait_ge(reduced, 6 * t + (p - 1))
                nc.scalar.activation(relu_ab[:, s, :], acc[:, s, :], ACT.Relu).then_inc(relu_ready, 1)

            def zsum_to_sb(m):
                act.wait_ge(zsum_done, m + 1)
                nc.scalar.copy(z01[:, :], mlp[:, 0:TB]).then_inc(zsum_sb, 1)
                nc.scalar.copy(z2d[0:MAPS, :], mlp[0:MAPS, TB:2 * TB]).then_inc(zsum_sb, 1)

            def h1_to_sb(m):
                act.wait_ge(h1_done, m + 1)
                for c in range(H1 // P):
                    nc.scalar.activation(h1[:, c, :], mlp[:, c * TB:(c + 1) * TB], ACT.Relu,
                                         bias=bt1[:, c:c + 1]).then_inc(h1_sb, 1)

            def h2_to_sb(m):
                act.wait_ge(h2_done, m + 1)
                for c in range(H2 // P):
                    nc.scalar.activation(h2[:, c, :], mlp[:, c * TB:(c + 1) * TB], ACT.Relu,
                                         bias=bt2[:, c:c + 1]).then_inc(h2_sb, 1)

            def y_to_sb(m):
                act.wait_ge(y_done, m + 1)
                if not is_first(m):
                    act.wait_ge(out_done, 16 * m)
                nc.scalar.copy(y_sb[:, :], mlp[0:1, 0:TB]).then_inc(y_ready, 1)

            act.wait_ge(const_in, const_count)
            transposes_to_sb(0)
            base_to_ps(0, 0)

            def tile(t, ahead=True):
                zero = is_first(t)
                base_to_ps(t, 1)
                evacuate(t, 0)
                evacuate(t, 1)
                if not zero:
                    zsum_to_sb(t - 1)
                evacuate(t, 2)
                if not zero:
                    h1_to_sb(t - 1)
                evacuate(t, 3)
                if ahead:
                    transposes_to_sb(t + 1)
                if not zero:
                    h2_to_sb(t - 1)
                evacuate(t, 4)
                if not zero:
                    y_to_sb(t - 1)
                if ahead:
                    base_to_ps(t + 1, 0)
                evacuate(t, 5)

            tile(0)
            with act.Fori(1, TILES - 2) as t:
                tile(t)
            tile(TILES - 2)
            tile(TILES - 1, ahead=False)
            zsum_to_sb(TILES - 1)
            h1_to_sb(TILES - 1)
            h2_to_sb(TILES - 1)
            y_to_sb(TILES - 1)

        @block.tensor
        def _(pe):
            def transpose(t):
                pe.wait_ge(gathered, 16 * FIELDS * (t + 1))
                if not is_first(t):
                    pe.wait_ge(x0t_ready, t)
                for g in range(FIELDS * DIM // P):
                    last = nc.tensor.transpose(stage[:, g, :], emb[:, g * P:(g + 1) * P], eye_sb[:, :])
                last.then_inc(transposed, 1)

            def phase(t, p):
                s, layer = PHASES[p]
                plan = plan_of(t)
                order = plan.phases[p][2]
                if not (is_first(t) and p < 2):
                    pe.wait_ge(relu_ready, 6 * t + (p - 1))
                for i, (who, n, j, w) in enumerate(order):
                    pe.wait_ge(zd_ready if who == "dve" else zg_ready, count(who, t, n + 1))
                    slot = plan.slot(who, n)
                    for c in range(w):
                        weights = w0[:, j + c, :] if layer == 0 else w12_sb[:, layer - 1, j + c, :]
                        for h in range(2):
                            z = zd[:, slot, c, :] if who == "dve" else zg[:, slot, :]
                            last = nc.tensor.matmul(acc[h * MAPS:(h + 1) * MAPS, s, :], weights,
                                                    z[:, h * HALF:(h + 1) * HALF],
                                                    start=(i == 0 and c == 0),
                                                    stop=(i == len(order) - 1 and c == w - 1))
                    last.then_inc(zd_used if who == "dve" else zg_used, 1)
                    if layer == 0 and i == 0:
                        pe.wait_ge(squares_ready, 2 * t + (s + 1))
                        for h in range(2):
                            nc.tensor.matmul(acc[h * MAPS:(h + 1) * MAPS, s, :], w0[:, L0CH, :],
                                             xk_sb[:, s, h * HALF:(h + 1) * HALF], start=False, stop=False)

            def zsum(m):
                pe.wait_ge(reduced, 6 * (m + 1))
                if not is_first(m):
                    pe.wait_ge(y_ready, m)
                for dst, layer in ((mlp[0:MAPS, 0:TB], 0), (mlp[MAPS:P, 0:TB], 1), (mlp[0:MAPS, TB:2 * TB], 2)):
                    for s in range(2):
                        last = nc.tensor.matmul(dst, eye2_sb[:, :], zpart[:, layer, s, :],
                                                start=(s == 0), stop=(s == 1))
                last.then_inc(zsum_done, 1)

            def mlp1(m):
                pe.wait_ge(zsum_sb, 2 * (m + 1))
                if not is_first(m):
                    pe.wait_ge(dense_in, 16 * m)
                for c in range(H1 // P):
                    dst = mlp[:, c * TB:(c + 1) * TB]
                    nc.tensor.matmul(dst, wt1a[:, c * P:(c + 1) * P], z01[:, :], start=True, stop=False)
                    last = nc.tensor.matmul(dst, wt1b[:, c * P:(c + 1) * P], z2d[:, :], start=False, stop=True)
                last.then_inc(h1_done, 1)

            def mlp2(m):
                pe.wait_ge(h1_sb, 4 * (m + 1))
                for c in range(H2 // P):
                    for k in range(H1 // P):
                        last = nc.tensor.matmul(mlp[:, c * TB:(c + 1) * TB], wt2[:, k, c * P:(c + 1) * P],
                                                h1[:, k, :], start=(k == 0), stop=(k == H1 // P - 1))
                last.then_inc(h2_done, 1)

            def mlp3(m):
                pe.wait_ge(h2_sb, 2 * (m + 1))
                for k in range(H2 // P):
                    last = nc.tensor.matmul(mlp[0:1, 0:TB], wt3[:, k:k + 1], h2[:, k, :],
                                            start=(k == 0), stop=(k == H2 // P - 1))
                last.then_inc(y_done, 1)

            pe.wait_ge(const_in, const_count)
            transpose(0)
            pe.wait_ge(w0_ready, 1)

            def tile(t, ahead=True):
                zero = is_first(t)
                phase(t, 0)
                phase(t, 1)
                if not zero:
                    zsum(t - 1)
                phase(t, 2)
                if not zero:
                    mlp1(t - 1)
                phase(t, 3)
                if ahead:
                    transpose(t + 1)
                if not zero:
                    mlp2(t - 1)
                phase(t, 4)
                if not zero:
                    mlp3(t - 1)
                phase(t, 5)

            tile(0)
            with pe.Fori(1, TILES - 2) as t:
                tile(t)
            tile(TILES - 2)
            tile(TILES - 1, ahead=False)
            zsum(TILES - 1)
            mlp1(TILES - 1)
            mlp2(TILES - 1)
            mlp3(TILES - 1)


def layout(inputs):
    p = np.arange(P)
    base = np.array(BASES)
    m = (base[:, None] + p[None, :] % 4 + p[None, :] // 4) % FIELDS
    h = np.broadcast_to(p % MAPS, m.shape)
    w12 = np.stack([np.asarray(inputs[f"L0_rec_W{n}"])[m, h].transpose(1, 0, 2) for n in (1, 2)])
    W0 = np.asarray(inputs["L0_rec_W0"])
    h0 = np.broadcast_to(p // 4, m.shape)
    w0a = W0[m, h0].transpose(1, 0, 2)[:, 0:L0CH]
    w0b = W0[h0, m].transpose(1, 0, 2)[:, 0:L0CH]
    w0c = W0[np.arange(FIELDS), np.arange(FIELDS)]
    return {
        "ids": np.asarray(inputs["ids"]),
        "dense_t": np.asarray(inputs["dense_ctx"]).T,
        **{f"tbl_{f}": np.asarray(inputs[f"tbl_{f}"]) for f in range(FIELDS)},
        "w0a": w0a, "w0b": w0b, "w0c": w0c, "w12": w12,
        "wtop1": np.asarray(inputs["W_top1"]), "btop1": np.asarray(inputs["b_top1"]).reshape(-1, P).T,
        "wtop2": np.asarray(inputs["W_top2"]), "btop2": np.asarray(inputs["b_top2"]).reshape(-1, P).T,
        "wtop3": np.asarray(inputs["W_top3"]).reshape(-1, P).T,
        "eye": np.eye(P, dtype=np.float32), "eye2": np.tile(np.eye(MAPS, dtype=np.float32), (2, 1)),
    }


def kernel(**inputs):
    from concourse import bacc
    from concourse.bass_utils import run_bass_kernel_spmd

    arrays = {f"{k}_in": np.ascontiguousarray(v) for k, v in layout(inputs).items()}
    nc = bacc.Bacc("TRN2", target_bir_lowering=False, num_devices=1,
                   dynamic_dma_scratch_size=DMA_RING)
    aps = {k[:-3]: nc.dram_tensor(k, v.shape, mybir.dt.from_np(v.dtype), kind="ExternalInput").ap()
           for k, v in arrays.items()}
    out = nc.dram_tensor("y_out", (BATCH, 1), F32, kind="ExternalOutput").ap()
    tables = [aps.pop(f"tbl_{f}") for f in range(FIELDS)]
    build_cin_tower(nc, tables=tables, out=out, **aps)
    r = run_bass_kernel_spmd(nc, [arrays], core_ids=[0])
    return r.results[0]["y_out"]
```

```python
from contextlib import ExitStack

import numpy as np

import concourse.bass as bass
from concourse import mybir

F32 = mybir.dt.float32
I32 = mybir.dt.int32
U32 = mybir.dt.uint32
ALU = mybir.AluOpType
ACT = mybir.ActivationFunctionType
AX_X = mybir.AxisListType.X

P = 128
FIELDS = 32
DIM = 16
BATCH = 1024
MAPS = 64
TB = 128
TILES = BATCH // TB
HALF = 512
STREAM = 2 * HALF
COLS = TB * DIM
NCH = FIELDS * MAPS // P
BASES = [1, 5, 9, 13, 0, 2, 3, 4, 6, 7, 8, 10, 11, 12, 14, 15]
L0CH = 4
H1, H2 = 512, 256
DENSE = 16
ZD_ROWS = MAPS + DENSE

PHASES = [(0, 0), (1, 0), (0, 1), (1, 1), (0, 2), (1, 2)]
POOL_CHUNKS = [0, 0, 4, 2, 4, 2]
POOL_CHUNKS_FIRST = [0, 0, 2, 4, 4, 2]
WARM_PRODUCTS = 5
ZD_BUFS = 3
ZG_BUFS = 4
GATHERS_NEXT = {3: 7, 5: 5}
GATHERS_LATER = {9: 2, 11: 18}
DMA_RING = 8192


class Plan:

    def __init__(self, pool_chunks, like=None, pool_last=()):
        self.phases = []
        nd = ng = 0
        for p, (_, layer) in enumerate(PHASES):
            n = L0CH if layer == 0 else NCH
            first_pool = n - pool_chunks[p]
            dve = [("dve", nd + i, j, min(2, first_pool - j)) for i, j in enumerate(range(0, first_pool, 2))]
            pool = [("pool", ng + i, j, 1) for i, j in enumerate(range(first_pool, n))]
            order, taken = [], 0
            for i, item in enumerate(dve):
                order.append(item)
                while p not in pool_last and taken < len(pool) and (taken + 1) * len(dve) <= (i + 1) * (len(pool) + 1):
                    order.append(pool[taken])
                    taken += 1
            self.phases.append((dve, pool, order + pool[taken:]))
            nd += len(dve)
            ng += len(pool)
        self.total = {"dve": nd, "pool": ng}
        self.steady = self.total if like is None else like.total
        self.end = {who: [sum(len(x[k]) for x in self.phases[:p + 1]) for p in range(6)]
                    for k, who in enumerate(("dve", "pool"))}

    def slot(self, who, n):
        bufs = ZD_BUFS if who == "dve" else ZG_BUFS
        return (n + self.steady[who] - self.total[who]) % bufs


STEADY = Plan(POOL_CHUNKS)
FIRST = Plan(POOL_CHUNKS_FIRST, like=STEADY, pool_last=(2,))


def is_first(t):
    return isinstance(t, int) and t == 0


def plan_of(t):
    return FIRST if is_first(t) else STEADY


def count(who, t, n):
    if is_first(t):
        return n
    return STEADY.total[who] * t + (FIRST.total[who] - STEADY.total[who] + n)


def freed_at(who, t, n):
    plan = plan_of(t)
    slot = plan.slot(who, n)
    before = [x for x in range(n) if plan.slot(who, x) == slot]
    if before:
        return count(who, t, before[-1] + 1)
    if is_first(t):
        return None
    last = max(x for x in range(STEADY.total[who]) if STEADY.slot(who, x) == slot)
    return count(who, t, last + 1 - STEADY.total[who])


def build_cin_tower(nc, ids, dense_t, tables, w0a, w0b, w0c, w12, wtop1, btop1, wtop2, btop2, wtop3,
                    eye, eye2, select, out):
    with ExitStack() as ctx:
        def sb(name, shape, dt=F32):
            return ctx.enter_context(nc.sbuf_tensor(name, shape, dt))

        def psum(name, shape):
            return ctx.enter_context(nc.psum_tensor(name, shape, F32))

        def sem(name):
            return ctx.enter_context(nc.semaphore(name))

        rolled = sb("rolled", [P, NCH, COLS])
        zd = sb("zd", [P, ZD_BUFS, 2, STREAM])
        zg = sb("zg", [P, ZG_BUFS, STREAM])
        xk_sb = sb("xk_sb", [P, 2, STREAM])
        relu_ab = sb("relu_ab", [P, 2, HALF])
        x0t = sb("x0t", [P, FIELDS * DIM // P, TB])
        emb = sb("emb", [P, FIELDS * DIM])
        ids_sb = sb("ids_sb", [P, TILES, FIELDS], I32)
        ids_tile = sb("ids_tile", [P, FIELDS], I32)
        w0 = sb("w0", [P, L0CH + 1, MAPS])
        w0rev = sb("w0rev", [P, L0CH, MAPS])
        w12_sb = sb("w12_sb", [P, 2, NCH, MAPS])
        wt1a = sb("wt1a", [P, H1])
        wt1b = sb("wt1b", [ZD_ROWS, H1])
        wt2 = sb("wt2", [P, H1 // P, H2])
        wt3 = sb("wt3", [P, H2 // P])
        bt1 = sb("bt1", [P, H1 // P])
        bt2 = sb("bt2", [P, H2 // P])
        eye_sb = sb("eye_sb", [P, P])
        eye2_sb = sb("eye2_sb", [P, MAPS])
        zpart = sb("zpart", [P, 3, 2, TB])
        z01 = sb("z01", [P, TB])
        z2d = sb("z2d", [ZD_ROWS, TB])
        h1 = sb("h1", [P, H1 // P, TB])
        h2 = sb("h2", [P, H2 // P, TB])
        y_sb = sb("y_sb", [1, TB])

        head_x0 = zg[:, 3, 0:HALF]
        head_select = zg[:, 1:3, :].rearrange("r a c -> r (a c)")[:, 0:(L0CH + 1) * 2 * P].rearrange(
            "r (j h p) -> r j h p", h=2, p=P)

        acc = psum("acc", [P, 2, HALF])
        xk_ps = psum("xk_ps", [P, 2, STREAM])
        stage = psum("stage", [P, FIELDS * DIM // P, TB])
        mlp = psum("mlp", [P, HALF])

        scratch = nc.dram_tensor("x0_scratch", [2, FIELDS, DIM, TB], F32, kind="Internal").ap()

        out_row = out.rearrange("b o -> o b")

        const_in = sem("const_in")
        const_count = 16 * 18
        head_transposed = sem("head_transposed")
        head_x0_ready = sem("head_x0_ready")
        head_picked = sem("head_picked")
        head_rolled = sem("head_rolled")
        w0_zeroed = sem("w0_zeroed")
        w0_ready = sem("w0_ready")
        act_warm = sem("act_warm")
        ids_in = sem("ids_in")
        later_ids_in = sem("later_ids_in")
        ids_copied = sem("ids_copied")
        gathered = sem("gathered")
        first_gathered = [sem(f"first_gathered{g}") for g in range(FIELDS * DIM // P)]
        transposed = sem("transposed")
        x0t_ready = sem("x0t_ready")
        base_in = [sem("base_x_in"), sem("base_y_in")]
        base_ps = sem("base_ps")
        squares_ready = sem("squares_ready")
        scratch_in = sem("scratch_in")
        rolled_in = [[sem(f"rolled_{'xy'[s]}{j}_in") for j in range(NCH)] for s in range(2)]
        zd_ready = sem("zd_ready")
        zd_used = sem("zd_used")
        zg_ready = sem("zg_ready")
        zg_used = sem("zg_used")
        xk_ps_ready = sem("xk_ps_ready")
        xk_sb_ready = sem("xk_sb_ready")
        relu_ready = sem("relu_ready")
        reduced = sem("reduced")
        dense_in = sem("dense_in")
        zsum_done = sem("zsum_done")
        zsum_sb = sem("zsum_sb")
        h1_done = sem("h1_done")
        h1_sb = sem("h1_sb")
        h2_done = sem("h2_done")
        h2_sb = sem("h2_sb")
        y_done = sem("y_done")
        last_z01_done = sem("last_z01_done")
        last_z01_sb = sem("last_z01_sb")
        last_z2_done = sem("last_z2_done")
        last_z2_sb = sem("last_z2_sb")
        last_h1_done = sem("last_h1_done")
        last_h1_sb = sem("last_h1_sb")
        last_h2_done = sem("last_h2_done")
        last_h2_sb = sem("last_h2_sb")
        y_ready = sem("y_ready")
        out_done = sem("out_done")

        block = ctx.enter_context(nc.Block())

        def twice(x, w):
            return bass.AP(x.tensor, x.offset, [x.ap[0], [0, w], x.ap[-1]])

        def head_bank(j, h):
            if j % 2 == 0:
                return xk_ps[:, 1, h * HALF:(h + 1) * HALF]
            if j == 1:
                return acc[:, h, :]
            return (stage[:, :, :].rearrange("p g b -> p (g b)"), mlp[:, :])[h]

        last_h1_bank = [xk_ps[:, 0, 0:TB], xk_ps[:, 0, HALF:HALF + TB], stage[:, 0, :], acc[:, 0, 0:TB]]
        last_h2_bank = [mlp[:, 0:TB], acc[:, 1, 0:TB]]
        last_y_bank = xk_ps[0:1, 0, 0:TB]

        def wait_rolled(eng, t, s, j):
            if s == 0 and j < L0CH:
                if is_first(t):
                    eng.wait_ge(head_rolled, 2 * (j + 1))
                else:
                    eng.wait_ge(rolled_in[s][j], 16 * t)
            else:
                eng.wait_ge(rolled_in[s][j], 16 * (t + 1))

        @block.sync
        def _(sp):
            def known(value):
                return value if isinstance(value, int) else sp.snap(sp.to_reg(value))

            def at(t):
                return t * TB if isinstance(t, int) else sp.snap(t * TB)

            def load_dense(first):
                sp.dma_start(z2d[MAPS:ZD_ROWS, :], dense_t[:, bass.ds(first, TB)]).then_inc(dense_in, 16)

            def store_y(m):
                first = at(m)
                sp.wait_ge(y_ready, m + 1)
                sp.dma_start(out_row[:, bass.ds(first, TB)], y_sb[:, :]).then_inc(out_done, 16)

            def store_scratch(tiles):
                sp.wait_ge(x0t_ready, tiles)
                for copy in range(2):
                    sp.dma_start(scratch[copy].rearrange("(g f) d b -> (f d) g b", g=x0t.shape[1]),
                                 x0t[:, :, :]).then_inc(scratch_in, 16)

            def rows_from(first, s, step):
                return bass.AP(scratch.tensor, scratch.offset + first * COLS + s * STREAM,
                               [[COLS, FIELDS], [step * COLS, 4], [1, STREAM]])

            def load_base(s):
                sp.dma_start(xk_sb[:, s, :], rows_from(0, s, 0)).then_inc(base_in[s], 16)

            def load_rolled(s, j):
                sp.dma_start(rolled[:, j, s * STREAM:(s + 1) * STREAM],
                             rows_from(BASES[j], s, 1)).then_inc(rolled_in[s][j], 16)

            first = L0CH
            load_order = ([(0, j) for j in range(-1, first)] + [(1, j) for j in range(-1, first)]
                          + [(0, j) for j in range(first, NCH)] + [(1, j) for j in range(first, NCH)])

            sp.dma_start(ids_sb[:, 0, :], ids[0:TB, :]).then_inc(ids_in, 16)
            sp.dma_start(ids_sb[:, 1:, :], ids[TB:, :].rearrange("(t b) f -> b t f", b=TB)
                         ).then_inc(later_ids_in, 16)
            sp.dma_start(eye_sb[:, :], eye).then_inc(const_in, 16)
            sp.dma_start(head_select, select).then_inc(const_in, 16)
            sp.wait_ge(w0_zeroed, 2)
            sp.dma_start(w0[:, 0:L0CH, :], w0a).then_inc(const_in, 16)
            sp.dma_start(w0rev[:, 0:L0CH - 1, :], w0b[:, 0:L0CH - 1, :]).then_inc(const_in, 16)
            for q in range(3):
                sp.dma_start(w0rev[q:P:4, L0CH - 1, :], w0b[q:P:4, L0CH - 1, :]).then_inc(const_in, 16)
            sp.dma_start(w0[0:P:4, L0CH, :], w0c).then_inc(const_in, 16)
            sp.dma_start(w12_sb[:, 0, :, :], w12[0]).then_inc(const_in, 16)
            sp.dma_start(w12_sb[:, 1, :, :], w12[1]).then_inc(const_in, 16)
            sp.dma_start(wt1a[:, :], wtop1[0:P, :]).then_inc(const_in, 16)
            sp.dma_start(wt1b[:, :], wtop1[P:P + ZD_ROWS, :]).then_inc(const_in, 16)
            sp.dma_start(wt2[:, :, :], wtop2.rearrange("(c p) n -> p c n", p=P)).then_inc(const_in, 16)
            sp.dma_start(wt3[:, :], wtop3).then_inc(const_in, 16)
            sp.dma_start(bt1[:, :], btop1).then_inc(const_in, 16)
            sp.dma_start(bt2[:, :], btop2).then_inc(const_in, 16)
            sp.dma_start(eye2_sb[:, :], eye2).then_inc(const_in, 16)
            sp.dma_start(z2d[MAPS:ZD_ROWS, :], dense_t[:, 0:TB]).then_inc(const_in, 16)
            store_scratch(1)
            sp.wait_ge(scratch_in, 32)
            rest = []
            for s in range(2):
                pool_first = NCH - POOL_CHUNKS_FIRST[2 + s]
                rest += [(s, j) for j in (*range(pool_first, NCH), *range(first, pool_first))]
            for s, j in [(1, j) for j in range(-1, first)] + rest:
                if j < 0:
                    load_base(s)
                else:
                    load_rolled(s, j)

            def tile(t, ahead=True):
                if ahead:
                    dve_count, pool_count, x0t_count = (
                        known(count("dve", t, plan_of(t).end["dve"][3])),
                        known(count("pool", t, plan_of(t).end["pool"][3])), known(t + 2))
                    sp.wait_ge(zd_ready, dve_count)
                    sp.wait_ge(zg_ready, pool_count)
                    store_scratch(x0t_count)
                if not is_first(t):
                    first = at(t)
                    sp.wait_ge(h1_done, t)
                    load_dense(first)
                if ahead:
                    freed = {}
                    for s in range(2):
                        dve_items, pool_items, _ = plan_of(t).phases[4 + s]
                        for _, n, j, w in dve_items:
                            for c in range(w):
                                freed[(s, j + c)] = (zd_ready, count("dve", t, n + 1))
                        for _, n, j, _ in pool_items:
                            freed[(s, j)] = (zg_ready, count("pool", t, n + 1))
                    base_free = [known(count("pool", t, plan_of(t).end["pool"][4 + s])) for s in range(2)]
                    sp.wait_ge(scratch_in, 32 * (t + 2))
                    for s, j in load_order:
                        if j < 0:
                            sp.wait_ge(zg_ready, base_free[s])
                            load_base(s)
                        else:
                            sp.wait_ge(*freed[(s, j)])
                            load_rolled(s, j)
                if not is_first(t):
                    store_y(t - 1)

            tile(0)
            with sp.Fori(1, TILES - 2) as t:
                tile(t)
            tile(TILES - 2)
            tile(TILES - 1, ahead=False)
            store_y(TILES - 1)
            sp.wait_ge(out_done, 16 * TILES)

        @block.gpsimd
        def _(pool):
            def gather(index, f, landed=gathered):
                pool.indirect_dma_start(emb[:, f * DIM:(f + 1) * DIM], None, tables[f],
                                        bass.IndirectOffsetOnAxis(index[:, f:f + 1].bitcast(U32), 0)
                                        ).then_inc(landed, 16)

            def product(t, p, n, j):
                s, layer = PHASES[p]
                free = freed_at("pool", t, n)
                if free is not None:
                    pool.wait_ge(zg_used, free)
                if layer == 1 or is_first(t):
                    wait_rolled(pool, t, s, j)
                nc.gpsimd.tensor_tensor(zg[:, plan_of(t).slot("pool", n), :],
                                        rolled[:, j, s * STREAM:(s + 1) * STREAM],
                                        xk_sb[:, s, :], ALU.mult).then_inc(zg_ready, 1)

            pool.wait_ge(ids_in, 16)
            for f in range(FIELDS):
                gather(ids_sb[:, 0, :], f, landed=first_gathered[f * DIM // P])
            pool.wait_ge(transposed, 1)
            pool.wait_ge(head_transposed, 1)
            pool.wait_ge(later_ids_in, 16)
            for f in range(FIELDS):
                gather(ids_sb[:, 1, :], f)

            def tile(t, later=True, following=True):
                plan = plan_of(t)
                start = min(GATHERS_LATER)
                for p in range(2, 6):
                    if plan.phases[p][1]:
                        pool.wait_ge(xk_sb_ready, 16 * t + 4 * (p - 1))
                    for _, n, j, _ in plan.phases[p][1]:
                        place = n + STEADY.total["pool"] - plan.total["pool"]
                        if later and place == start - 1:
                            pool.wait_ge(gathered, 16 * FIELDS * (t + 1))
                        if later and place == start:
                            pool.wait_ge(ids_copied, t + 1)
                            pool.wait_ge(transposed, t + 2)
                        product(t, p, n, j)
                        if later and place == start - 1:
                            nc.gpsimd.tensor_copy(ids_tile[:, :], ids_sb[:, t + 2, :]).then_inc(ids_copied, 1)
                        if following and place in GATHERS_NEXT:
                            done = sum(GATHERS_LATER.values()) + sum(
                                k for x, k in GATHERS_NEXT.items() if x < place)
                            for f in range(done, done + GATHERS_NEXT[place]):
                                gather(ids_tile, f)
                        if later and place in GATHERS_LATER:
                            done = sum(k for x, k in GATHERS_LATER.items() if x < place)
                            for f in range(done, done + GATHERS_LATER[place]):
                                gather(ids_tile, f)

            tile(0, following=False)
            with pool.Fori(1, TILES - 2) as t:
                tile(t)
            tile(TILES - 2, later=False)
            tile(TILES - 1, later=False, following=False)

        @block.vector
        def _(dve):
            nc.vector.memset(w0[:, L0CH, :], 0.0).then_inc(w0_zeroed, 1)
            nc.vector.memset(w0rev[:, L0CH - 1, :], 0.0).then_inc(w0_zeroed, 1)
            dve.wait_ge(const_in, const_count)
            nc.vector.tensor_tensor(w0[:, 0:L0CH, :], w0[:, 0:L0CH, :], w0rev[:, :, :],
                                    ALU.add).then_inc(w0_ready, 1)

            dve.wait_ge(head_transposed, 1)
            nc.vector.tensor_copy(head_x0[:, :], acc[:, 0, :]).then_inc(head_x0_ready, 1)

            def reduce_d(t, p):
                s, layer = PHASES[p]
                dve.wait_ge(relu_ready, 6 * t + (p + 1))
                nc.vector.tensor_reduce(zpart[:, layer, s, :],
                                        relu_ab[:, s, :].rearrange("p (d b) -> p b d", b=TB),
                                        AX_X, ALU.add).then_inc(reduced, 1)

            def tile(t):
                y0, x1, y1, x2, y2 = plan_of(t).end["dve"][0:5]
                reduces = {y0 + 1: (t - 1, 5), x1 + 4: (t, 0), y1: (t, 1), y1 + 3: (t, 2), x2 + 3: (t, 3),
                           y2 + 3: (t, 4)}
                for p, (s, layer) in enumerate(PHASES):
                    if layer == 0:
                        dve.wait_ge(base_ps, 4 * t + 2 * (s + 1))
                        if is_first(t) and s == 0:
                            dve.wait_ge(squares_ready, 1)
                    else:
                        dve.wait_ge(xk_ps_ready, 16 * t + 4 * (p - 1))
                    for _, n, j, w in plan_of(t).phases[p][0]:
                        free = freed_at("dve", t, n)
                        if free is not None:
                            dve.wait_ge(zd_used, free)
                        for c in range(j, j + w):
                            if layer == 0 or (layer == 1 and c >= L0CH):
                                wait_rolled(dve, t, s, c)
                        nc.vector.tensor_tensor(zd[:, plan_of(t).slot("dve", n), 0:w, :],
                                                rolled[:, j:j + w, s * STREAM:(s + 1) * STREAM],
                                                twice(xk_ps[:, s, :], w), ALU.mult).then_inc(zd_ready, 1)
                        if n in reduces and not (is_first(t) and reduces[n][1] == 5):
                            if reduces[n][1] == 0 and not is_first(t):
                                dve.wait_ge(zsum_done, t)
                            reduce_d(*reduces[n])

            tile(0)
            with dve.Fori(1, TILES - 2) as t:
                tile(t)
            tile(TILES - 2)
            tile(TILES - 1)
            reduce_d(TILES - 1, 5)

        @block.scalar
        def _(act):
            def transposes_to_sb(t):
                act.wait_ge(transposed, t + 1)
                if not is_first(t):
                    act.wait_ge(scratch_in, 32 * t)
                nc.scalar.copy(x0t[:, :, :], stage[:, :, :]).then_inc(x0t_ready, 1)

            def base_to_ps(t, s):
                if not is_first(t):
                    act.wait_ge(zd_ready, count("dve", t, STEADY.end["dve"][4 + s] - STEADY.end["dve"][5]))
                act.wait_ge(base_in[s], 16 * (t + s))
                for h in range(2):
                    nc.scalar.copy(xk_ps[:, s, h * HALF:(h + 1) * HALF],
                                   xk_sb[:, s, h * HALF:(h + 1) * HALF]).then_inc(base_ps, 1)
                act.wait_ge(base_ps, 4 * t + 2 * (s + 1))
                nc.scalar.activation(xk_sb[:, s, :], xk_sb[:, s, :], ACT.Square).then_inc(squares_ready, 1)

            def evacuate(t, p):
                s, layer = PHASES[p]
                who, n, _, _ = plan_of(t).phases[p][2][-1]
                act.wait_ge(zd_used if who == "dve" else zg_used, count(who, t, n + 1))
                if layer < 2:
                    for dst, ready in ((xk_ps, xk_ps_ready), (xk_sb, xk_sb_ready)):
                        for h in range(2):
                            for copy in range(2):
                                nc.scalar.activation(
                                    dst[copy * MAPS:(copy + 1) * MAPS, s, h * HALF:(h + 1) * HALF],
                                    acc[h * MAPS:(h + 1) * MAPS, s, :], ACT.Relu).then_inc(ready, 1)
                if not (is_first(t) and p < 2):
                    act.wait_ge(reduced, 6 * t + (p - 1))
                nc.scalar.activation(relu_ab[:, s, :], acc[:, s, :], ACT.Relu).then_inc(relu_ready, 1)

            def zsum_to_sb(m):
                act.wait_ge(zsum_done, m + 1)
                nc.scalar.copy(z01[:, :], mlp[:, 0:TB]).then_inc(zsum_sb, 1)
                nc.scalar.copy(z2d[0:MAPS, :], mlp[0:MAPS, TB:2 * TB]).then_inc(zsum_sb, 1)

            def h1_to_sb(m):
                act.wait_ge(h1_done, m + 1)
                for c in range(H1 // P):
                    nc.scalar.activation(h1[:, c, :], mlp[:, c * TB:(c + 1) * TB], ACT.Relu,
                                         bias=bt1[:, c:c + 1]).then_inc(h1_sb, 1)

            def h2_to_sb(m):
                act.wait_ge(h2_done, m + 1)
                for c in range(H2 // P):
                    nc.scalar.activation(h2[:, c, :], mlp[:, c * TB:(c + 1) * TB], ACT.Relu,
                                         bias=bt2[:, c:c + 1]).then_inc(h2_sb, 1)

            def y_to_sb(m):
                act.wait_ge(y_done, m + 1)
                if not is_first(m):
                    act.wait_ge(out_done, 16 * m)
                nc.scalar.copy(y_sb[:, :], mlp[0:1, 0:TB]).then_inc(y_ready, 1)

            act.wait_ge(const_in, const_count)
            nc.scalar.activation(y_sb[0:1, 0:1], bt1[0:1, 0:1], ACT.Relu).then_inc(act_warm, 1)
            transposes_to_sb(0)

            def head_chunk(j):
                for h in range(2):
                    act.wait_ge(head_picked, 2 * j + h + 1)
                    nc.scalar.copy(rolled[:, j, h * HALF:(h + 1) * HALF], head_bank(j, h)
                                   ).then_inc(head_rolled, 1)

            act.wait_ge(base_ps, 2)
            nc.scalar.activation(xk_sb[:, 0, :], xk_ps[:, 0, :], ACT.Square).then_inc(squares_ready, 1)
            head_chunk(0)
            head_chunk(1)
            head_chunk(2)
            head_chunk(3)
            act.wait_ge(head_rolled, 2 * L0CH)
            act.wait_ge(act_warm, 1)

            def tile(t, ahead=True):
                zero = is_first(t)
                base_to_ps(t, 1)
                evacuate(t, 0)
                evacuate(t, 1)
                if not zero:
                    zsum_to_sb(t - 1)
                evacuate(t, 2)
                if not zero:
                    h1_to_sb(t - 1)
                evacuate(t, 3)
                if ahead:
                    transposes_to_sb(t + 1)
                if not zero:
                    h2_to_sb(t - 1)
                evacuate(t, 4)
                if not zero:
                    y_to_sb(t - 1)
                if ahead:
                    base_to_ps(t + 1, 0)
                else:
                    act.wait_ge(last_z01_done, 1)
                    nc.scalar.copy(z01[:, :], stage[:, 0, :]).then_inc(last_z01_sb, 1)
                evacuate(t, 5)

            tile(0)
            with act.Fori(1, TILES - 2) as t:
                tile(t)
            tile(TILES - 2)
            tile(TILES - 1, ahead=False)

            act.wait_ge(last_z2_done, 1)
            nc.scalar.copy(z2d[0:MAPS, :], mlp[0:MAPS, TB:2 * TB]).then_inc(last_z2_sb, 1)
            for c in range(H1 // P):
                act.wait_ge(last_h1_done, c + 1)
                nc.scalar.activation(h1[:, c, :], last_h1_bank[c], ACT.Relu, bias=bt1[:, c:c + 1]
                                     ).then_inc(last_h1_sb, 1)
            for c in range(H2 // P):
                act.wait_ge(last_h2_done, c + 1)
                nc.scalar.activation(h2[:, c, :], last_h2_bank[c], ACT.Relu, bias=bt2[:, c:c + 1]
                                     ).then_inc(last_h2_sb, 1)
            act.wait_ge(y_done, TILES)
            act.wait_ge(out_done, 16 * (TILES - 1))
            nc.scalar.copy(y_sb[:, :], last_y_bank).then_inc(y_ready, 1)

        @block.tensor
        def _(pe):
            def transpose(t):
                if not is_first(t):
                    pe.wait_ge(gathered, 16 * FIELDS * t)
                    pe.wait_ge(x0t_ready, t)
                for g in range(FIELDS * DIM // P):
                    if is_first(t):
                        if g == FIELDS * DIM // P - 1:
                            for _ in range(WARM_PRODUCTS):
                                nc.tensor.matmul(mlp[:, :], eye_sb[:, :], w12_sb[:, 0, 0:HALF // MAPS, :],
                                                 start=True, stop=True)
                        pe.wait_ge(first_gathered[g], 16 * P // DIM)
                    last = nc.tensor.transpose(stage[:, g, :], emb[:, g * P:(g + 1) * P], eye_sb[:, :])
                last.then_inc(transposed, 1)

            def phase(t, p):
                s, layer = PHASES[p]
                plan = plan_of(t)
                order = plan.phases[p][2]
                if not (is_first(t) and p < 2):
                    pe.wait_ge(relu_ready, 6 * t + (p - 1))
                for i, (who, n, j, w) in enumerate(order):
                    pe.wait_ge(zd_ready if who == "dve" else zg_ready, count(who, t, n + 1))
                    slot = plan.slot(who, n)
                    for c in range(w):
                        weights = w0[:, j + c, :] if layer == 0 else w12_sb[:, layer - 1, j + c, :]
                        for h in range(2):
                            z = zd[:, slot, c, :] if who == "dve" else zg[:, slot, :]
                            last = nc.tensor.matmul(acc[h * MAPS:(h + 1) * MAPS, s, :], weights,
                                                    z[:, h * HALF:(h + 1) * HALF],
                                                    start=(i == 0 and c == 0),
                                                    stop=(i == len(order) - 1 and c == w - 1))
                    last.then_inc(zd_used if who == "dve" else zg_used, 1)
                    if layer == 0 and i == 0:
                        pe.wait_ge(squares_ready, 2 * t + (s + 1))
                        for h in range(2):
                            nc.tensor.matmul(acc[h * MAPS:(h + 1) * MAPS, s, :], w0[:, L0CH, :],
                                             xk_sb[:, s, h * HALF:(h + 1) * HALF], start=False, stop=False)

            def zsum(m):
                pe.wait_ge(reduced, 6 * (m + 1))
                if not is_first(m):
                    pe.wait_ge(y_ready, m)
                for dst, layer in ((mlp[0:MAPS, 0:TB], 0), (mlp[MAPS:P, 0:TB], 1), (mlp[0:MAPS, TB:2 * TB], 2)):
                    for s in range(2):
                        last = nc.tensor.matmul(dst, eye2_sb[:, :], zpart[:, layer, s, :],
                                                start=(s == 0), stop=(s == 1))
                last.then_inc(zsum_done, 1)

            def last_zsum01():
                pe.wait_ge(reduced, 6 * (TILES - 1) + 4)
                pe.wait_ge(x0t_ready, TILES)
                for dst, layer in ((stage[0:MAPS, 0, :], 0), (stage[MAPS:P, 0, :], 1)):
                    for s in range(2):
                        last = nc.tensor.matmul(dst, eye2_sb[:, :], zpart[:, layer, s, :],
                                                start=(s == 0), stop=(s == 1))
                last.then_inc(last_z01_done, 1)

            def mlp1(m):
                pe.wait_ge(zsum_sb, 2 * (m + 1))
                if not is_first(m):
                    pe.wait_ge(dense_in, 16 * m)
                for c in range(H1 // P):
                    dst = mlp[:, c * TB:(c + 1) * TB]
                    nc.tensor.matmul(dst, wt1a[:, c * P:(c + 1) * P], z01[:, :], start=True, stop=False)
                    last = nc.tensor.matmul(dst, wt1b[:, c * P:(c + 1) * P], z2d[:, :], start=False, stop=True)
                last.then_inc(h1_done, 1)

            def mlp2(m):
                pe.wait_ge(h1_sb, 4 * (m + 1))
                for c in range(H2 // P):
                    for k in range(H1 // P):
                        last = nc.tensor.matmul(mlp[:, c * TB:(c + 1) * TB], wt2[:, k, c * P:(c + 1) * P],
                                                h1[:, k, :], start=(k == 0), stop=(k == H1 // P - 1))
                last.then_inc(h2_done, 1)

            def mlp3(m):
                pe.wait_ge(h2_sb, 2 * (m + 1))
                for k in range(H2 // P):
                    last = nc.tensor.matmul(mlp[0:1, 0:TB], wt3[:, k:k + 1], h2[:, k, :],
                                            start=(k == 0), stop=(k == H2 // P - 1))
                last.then_inc(y_done, 1)

            pe.wait_ge(const_in, const_count)
            transpose(0)

            for d in range(4):
                last = nc.tensor.transpose(acc[:, 0, d * TB:(d + 1) * TB], emb[:, d:FIELDS * DIM:4], eye_sb[:, :])
            last.then_inc(head_transposed, 1)
            pe.wait_ge(head_x0_ready, 1)
            for h in range(2):
                nc.tensor.matmul(xk_ps[:, 0, h * HALF:(h + 1) * HALF], head_select[:, L0CH, h, :],
                                 head_x0[:, :], start=True, stop=True).then_inc(base_ps, 1)
            for j in range(L0CH):
                if j == 2:
                    pe.wait_ge(head_rolled, 2)
                if j == 3:
                    pe.wait_ge(x0t_ready, 1)
                for h in range(2):
                    nc.tensor.matmul(head_bank(j, h), head_select[:, j, h, :], head_x0[:, :],
                                     start=True, stop=True).then_inc(head_picked, 1)
            pe.wait_ge(w0_ready, 1)
            pe.wait_ge(head_rolled, 4)

            def tile(t, ahead=True):
                zero = is_first(t)
                phase(t, 0)
                phase(t, 1)
                if not zero:
                    zsum(t - 1)
                phase(t, 2)
                if not zero:
                    mlp1(t - 1)
                phase(t, 3)
                if ahead:
                    transpose(t + 1)
                if not zero:
                    mlp2(t - 1)
                phase(t, 4)
                if not zero:
                    mlp3(t - 1)
                if not ahead:
                    last_zsum01()
                phase(t, 5)

            tile(0)
            with pe.Fori(1, TILES - 2) as t:
                tile(t)
            tile(TILES - 2)
            tile(TILES - 1, ahead=False)

            pe.wait_ge(last_z01_sb, 1)
            pe.wait_ge(relu_ready, 6 * (TILES - 1) + 5)
            for c in range(H1 // P):
                nc.tensor.matmul(last_h1_bank[c], wt1a[:, c * P:(c + 1) * P], z01[:, :], start=True, stop=False)
            pe.wait_ge(y_ready, TILES - 1)
            pe.wait_ge(reduced, 6 * TILES)
            for s in range(2):
                last = nc.tensor.matmul(mlp[0:MAPS, TB:2 * TB], eye2_sb[:, :], zpart[:, 2, s, :],
                                        start=(s == 0), stop=(s == 1))
            last.then_inc(last_z2_done, 1)
            pe.wait_ge(dense_in, 16 * (TILES - 1))
            pe.wait_ge(last_z2_sb, 1)
            for c in range(H1 // P):
                nc.tensor.matmul(last_h1_bank[c], wt1b[:, c * P:(c + 1) * P], z2d[:, :],
                                 start=False, stop=True).then_inc(last_h1_done, 1)
            for k in range(H1 // P):
                pe.wait_ge(last_h1_sb, k + 1)
                for c in range(H2 // P):
                    last = nc.tensor.matmul(last_h2_bank[c], wt2[:, k, c * P:(c + 1) * P], h1[:, k, :],
                                            start=(k == 0), stop=(k == H1 // P - 1))
                    if k == H1 // P - 1:
                        last.then_inc(last_h2_done, 1)
            for k in range(H2 // P):
                pe.wait_ge(last_h2_sb, k + 1)
                last = nc.tensor.matmul(last_y_bank, wt3[:, k:k + 1], h2[:, k, :],
                                        start=(k == 0), stop=(k == H2 // P - 1))
            last.then_inc(y_done, 1)


def layout(inputs):
    p = np.arange(P)
    base = np.array(BASES)
    m = (base[:, None] + p[None, :] % 4 + p[None, :] // 4) % FIELDS
    h = np.broadcast_to(p % MAPS, m.shape)
    w12 = np.stack([np.asarray(inputs[f"L0_rec_W{n}"])[m, h].transpose(1, 0, 2) for n in (1, 2)])
    W0 = np.asarray(inputs["L0_rec_W0"])
    h0 = np.broadcast_to(p // 4, m.shape)
    w0a = W0[m, h0].transpose(1, 0, 2)[:, 0:L0CH]
    w0b = W0[h0, m].transpose(1, 0, 2)[:, 0:L0CH]
    w0c = W0[np.arange(FIELDS), np.arange(FIELDS)]
    fields = np.concatenate([m[0:L0CH], h0[0:1]])[:, None, :]
    select = (4 * fields + np.arange(2)[:, None] == p[:, None, None, None]).astype(np.float32)
    return {
        "ids": np.asarray(inputs["ids"]),
        "dense_t": np.asarray(inputs["dense_ctx"]).T,
        **{f"tbl_{f}": np.asarray(inputs[f"tbl_{f}"]) for f in range(FIELDS)},
        "w0a": w0a, "w0b": w0b, "w0c": w0c, "w12": w12,
        "wtop1": np.asarray(inputs["W_top1"]), "btop1": np.asarray(inputs["b_top1"]).reshape(-1, P).T,
        "wtop2": np.asarray(inputs["W_top2"]), "btop2": np.asarray(inputs["b_top2"]).reshape(-1, P).T,
        "wtop3": np.asarray(inputs["W_top3"]).reshape(-1, P).T,
        "select": select,
        "eye": np.eye(P, dtype=np.float32), "eye2": np.tile(np.eye(MAPS, dtype=np.float32), (2, 1)),
    }


def kernel(**inputs):
    from concourse import bacc
    from concourse.bass_utils import run_bass_kernel_spmd

    arrays = {f"{k}_in": np.ascontiguousarray(v) for k, v in layout(inputs).items()}
    nc = bacc.Bacc("TRN2", target_bir_lowering=False, num_devices=1,
                   dynamic_dma_scratch_size=DMA_RING)
    aps = {k[:-3]: nc.dram_tensor(k, v.shape, mybir.dt.from_np(v.dtype), kind="ExternalInput").ap()
           for k, v in arrays.items()}
    out = nc.dram_tensor("y_out", (BATCH, 1), F32, kind="ExternalOutput").ap()
    tables = [aps.pop(f"tbl_{f}") for f in range(FIELDS)]
    build_cin_tower(nc, tables=tables, out=out, **aps)
    r = run_bass_kernel_spmd(nc, [arrays], core_ids=[0])
    return r.results[0]["y_out"]
```
